# Optimizing a Trainium2 kernel written in Bass

```python
import numpy as np
import jax
import jax.numpy as jnp

def _softmax(x, axis=-1):
    return jax.nn.softmax(x, axis=axis)

def _gelu(x):
    return jax.nn.gelu(x, approximate=True)

def _silu(x):
    return jax.nn.silu(x)

def _sigmoid(x):
    return jax.nn.sigmoid(x)

def _layernorm(x, axis=-1, eps=1e-05):
    m = jnp.mean(x, axis=axis, keepdims=True)
    v = jnp.var(x, axis=axis, keepdims=True)
    return (x - m) / jnp.sqrt(v + eps)

def _scatter_add(tgt, idx, src, axis=0):
    return tgt.at[idx].add(src)

def _segment_sum(src, seg, n):
    return jax.ops.segment_sum(src, seg, n)
kernel_name = 'mk_adj_preln_d4_adj_r2_f6c5da'

def setup_inputs(seed: int=0):
    np.random.seed(seed)
    _w = jnp.asarray

    def _rec_inputs():
        import jax
        import jax.numpy as jnp
        _gk = jax.random.key(seed)
        x = -0.0005146 + 1 * jax.random.normal(jax.random.fold_in(_gk, 1), (8, 1024, 128), jnp.float32)
        _w = (1.0 + jnp.arange(1024, dtype=jnp.float32)) ** (-0.5)
        _w = _w / _w.mean()
        _pij = jnp.clip(0.015625 * _w[:, None] * _w[None, :], 0.0, 1.0)
        _a = jax.random.uniform(jax.random.fold_in(_gk, 2), (8, 1024, 1024)) < _pij
        adj = _a.astype(jnp.int32)
        return (x, adj)
    x, adj = _rec_inputs()

    def _L0_gnn_setup():
        import jax, jax.numpy as jnp
        import numpy as np
        B, N, C, OUT, S = (4, 1024, 128, 128, 25)
        DENSITY = 0.008
        key = jax.random.key(seed)
        kA, kX, kW = jax.random.split(key, 3)
        A = jax.random.bernoulli(kA, DENSITY, (B, N, N)).astype(jnp.int32)
        X = jax.random.normal(kX, (B, N, C), dtype=jnp.float32)
        W = jax.random.normal(kW, (2 * C, OUT), dtype=jnp.float32) * np.float32(1.0 / np.sqrt(2 * C))
        b = jnp.zeros((OUT,), dtype=jnp.float32)
        return {'A': A, 'X': X, 'W': W, 'b': b}
    _L0_gnn_all = _L0_gnn_setup()
    _L0_gnn_in = {k: v for k, v in _L0_gnn_all.items() if k in ('W', 'b')}
    del _L0_gnn_all

    def _L1_gnn_setup():
        import jax, jax.numpy as jnp
        import numpy as np
        B, N, F_IN, F_OUT = (8, 1024, 128, 128)
        ALPHA = 0.2
        NEG_BIG = -9000000000000000.0
        key = jax.random.key(seed)
        k1, k2, k3, k4 = jax.random.split(key, 4)
        x = jax.random.normal(k1, (B, N, F_IN), dtype=jnp.float32)
        adj = jax.random.randint(k2, (B, N, N), 0, 2, dtype=jnp.int32)
        gain = 1.414
        lim_W = gain * np.sqrt(6.0 / (F_IN + F_OUT))
        W = jax.random.uniform(k3, (F_IN, F_OUT), dtype=jnp.float32, minval=-lim_W, maxval=lim_W)
        lim_a = gain * np.sqrt(6.0 / (2 * F_OUT + 1))
        a = jax.random.uniform(k4, (2 * F_OUT, 1), dtype=jnp.float32, minval=-lim_a, maxval=lim_a)
        return {'x': x, 'adj': adj, 'W': W, 'a': a}
    _L1_gnn_all = _L1_gnn_setup()
    _L1_gnn_in = {k: v for k, v in _L1_gnn_all.items() if k in ('W', 'a')}
    del _L1_gnn_all

    def _L2_gnn_setup():
        import jax, jax.numpy as jnp
        import numpy as np
        NEG_INF = -1000000000.0
        LEAKY_SLOPE = 0.2
        key = jax.random.key(seed)
        k1, k2, k3, k4 = jax.random.split(key, 4)
        B, N, D_in, D_out = (8, 1024, 128, 128)
        x = jax.random.normal(k1, (B, N, D_in), dtype=jnp.float32)
        adj_matrix = jax.random.randint(k2, (B, N, N), 0, 2, dtype=jnp.int32)
        W = jax.random.normal(k3, (D_out, D_in), dtype=jnp.float32) / np.sqrt(D_in)
        a = jax.random.normal(k4, (1, 2 * D_out), dtype=jnp.float32) / np.sqrt(2 * D_out)
        return {'x': x, 'adj_matrix': adj_matrix, 'W': W, 'a': a}
    _L2_gnn_all = _L2_gnn_setup()
    _L2_gnn_in = {k: v for k, v in _L2_gnn_all.items() if k in ('W', 'a')}
    del _L2_gnn_all

    def _L3_gnn_setup():
        import jax, jax.numpy as jnp
        import numpy as np
        BS, N, D, R = (16, 256, 128, 2)
        key = jax.random.key(seed)
        ks = jax.random.split(key, 9)
        s = 1.0 / np.sqrt(D)
        return {'encoded_spans': jax.random.normal(ks[0], (BS, N, D), dtype=jnp.float32), 'w_rel1': jax.random.normal(ks[1], (R, D, D), dtype=jnp.float32) * s, 'w_root1': jax.random.normal(ks[2], (D, D), dtype=jnp.float32) * s, 'b1': jnp.zeros((D,), dtype=jnp.float32), 'w_rel2': jax.random.normal(ks[3], (R, D, D), dtype=jnp.float32) * s, 'w_root2': jax.random.normal(ks[4], (D, D), dtype=jnp.float32) * s, 'b2': jnp.zeros((D,), dtype=jnp.float32), 'aug_adj': jax.random.randint(ks[5], (BS, N, N), 0, 16, dtype=jnp.int64), 'punct_graph': jax.random.randint(ks[6], (BS, N, N), 0, 16, dtype=jnp.int64)}
    _L3_gnn_all = _L3_gnn_setup()
    _L3_gnn_in = {k: v for k, v in _L3_gnn_all.items() if k in ('w_rel1', 'w_root1', 'b1', 'w_rel2', 'w_root2', 'b2')}
    del _L3_gnn_all
    return {'x': x, 'adj': adj, 'L0_gnn_W': _L0_gnn_in['W'], 'L0_gnn_b': _L0_gnn_in['b'], 'L1_gnn_W': _L1_gnn_in['W'], 'L1_gnn_a': _L1_gnn_in['a'], 'L2_gnn_W': _L2_gnn_in['W'], 'L2_gnn_a': _L2_gnn_in['a'], 'L3_gnn_w_rel1': _L3_gnn_in['w_rel1'], 'L3_gnn_w_root1': _L3_gnn_in['w_root1'], 'L3_gnn_b1': _L3_gnn_in['b1'], 'L3_gnn_w_rel2': _L3_gnn_in['w_rel2'], 'L3_gnn_w_root2': _L3_gnn_in['w_root2'], 'L3_gnn_b2': _L3_gnn_in['b2']}

def reference(x, adj, L0_gnn_W, L0_gnn_b, L1_gnn_W, L1_gnn_a, L2_gnn_W, L2_gnn_a, L3_gnn_w_rel1, L3_gnn_w_root1, L3_gnn_b1, L3_gnn_w_rel2, L3_gnn_w_root2, L3_gnn_b2):
    import jax
    import jax.numpy as jnp

    def _L0_gnn_ref(A, X, W, b):
        import jax, jax.numpy as jnp
        import numpy as np
        B, N, C, OUT, S = (4, 1024, 128, 128, 25)
        DENSITY = 0.008
        mask = A != 0
        neg_inf = jnp.float32(-jnp.inf)
        pri = -jnp.arange(N, dtype=jnp.float32)
        scores = jnp.where(mask, pri, neg_inf)
        vals, idx = jax.lax.top_k(scores, S)
        valid = vals > neg_inf
        feats = jax.vmap(lambda x, i: x[i])(X, idx)
        feats = jnp.where(valid[..., None], feats, neg_inf)
        agg = feats.max(axis=2)
        degree = mask.sum(axis=-1)
        agg = jnp.where((degree <= S)[..., None], jnp.maximum(agg, 0.0), agg)
        h = jnp.concatenate([X, agg], axis=-1)
        out = jax.nn.relu(jnp.einsum('bnf,fo->bno', h, W) + b)
        return out

    def _L1_gnn_ref(x, adj, W, a):
        import jax, jax.numpy as jnp
        import numpy as np
        B, N, F_IN, F_OUT = (8, 1024, 128, 128)
        ALPHA = 0.2
        NEG_BIG = -9000000000000000.0
        h = jnp.einsum('bnf,fo->bno', x, W)
        a1 = a[:F_OUT, 0]
        a2 = a[F_OUT:, 0]
        s1 = h @ a1
        s2 = h @ a2
        e = jax.nn.leaky_relu(s1[:, :, None] + s2[:, None, :], negative_slope=ALPHA)
        att = jnp.where(adj > 0, e, jnp.float32(NEG_BIG))
        att = jax.nn.softmax(att, axis=1)
        h_prime = jnp.einsum('bij,bjo->bio', att, h)
        return jax.nn.elu(h_prime)

    def _L2_gnn_ref(x, adj_matrix, W, a):
        import jax, jax.numpy as jnp
        import numpy as np
        NEG_INF = -1000000000.0
        LEAKY_SLOPE = 0.2
        h = jnp.einsum('bnd,od->bno', x, W)
        D = h.shape[-1]
        a_left, a_right = (a[0, :D], a[0, D:])
        e = (h @ a_left)[:, :, None] + (h @ a_right)[:, None, :]
        e = jnp.where(e > 0, e, LEAKY_SLOPE * e)
        e = jnp.where(adj_matrix == 0, NEG_INF, e)
        alpha = jax.nn.softmax(e, axis=-1)
        return jnp.einsum('bij,bjd->bid', alpha, h)

    def _L3_gnn_ref(encoded_spans, w_rel1, w_root1, b1, w_rel2, w_root2, b2, aug_adj, punct_graph):
        import jax, jax.numpy as jnp
        import numpy as np
        BS, N, D, R = (16, 256, 128, 2)
        mask_punct = (punct_graph == 1) & (aug_adj != 1)
        mask_aug = aug_adj == 1
        masks = jnp.stack([mask_punct, mask_aug]).astype(encoded_spans.dtype)
        deg = jnp.maximum(masks.sum(axis=2), 1.0)[..., None]

        def conv(x, w_rel, w_root, b):
            out = jnp.einsum('bnd,de->bne', x, w_root) + b
            for r in range(R):
                agg = jnp.einsum('bij,bid->bjd', masks[r], x) / deg[r]
                out = out + jnp.einsum('bjd,de->bje', agg, w_rel[r])
            return out
        h = jax.nn.elu(conv(encoded_spans, w_rel1, w_root1, b1))
        h = jax.nn.elu(conv(h, w_rel2, w_root2, b2))
        return h
    h = jnp.maximum(_layernorm(x, axis=-1), 0.0)
    x = x + _L0_gnn_ref(adj, h, L0_gnn_W, L0_gnn_b)
    h = jnp.maximum(_layernorm(x, axis=-1), 0.0)
    x = x + _L1_gnn_ref(h, adj, L1_gnn_W, L1_gnn_a)
    h = jnp.maximum(_layernorm(x, axis=-1), 0.0)
    x = x + _L2_gnn_ref(h, adj, L2_gnn_W, L2_gnn_a)
    h = jnp.maximum(_layernorm(x, axis=-1), 0.0)
    x = x + _L3_gnn_ref(h, L3_gnn_w_rel1, L3_gnn_w_root1, L3_gnn_b1, L3_gnn_w_rel2, L3_gnn_w_root2, L3_gnn_b2, adj, adj)
    return x

_drawn_inputs = setup_inputs


def setup_inputs(seed=0):
    import zlib

    import numpy as np

    out = dict(_drawn_inputs(seed))
    spreads = {'L0_gnn_b': (0.0, 0.1), 'L3_gnn_b1': (0.0, 0.1), 'L3_gnn_b2': (0.0, 0.1)}
    factors = {'L2_gnn_a': 2.867}
    for name, (base, spread) in spreads.items():
        noise = np.random.default_rng([zlib.crc32(name.encode()), seed]).standard_normal(out[name].shape)
        drawn = base * np.exp(spread * noise) if base else spread * noise
        out[name] = jnp.asarray(drawn.astype(out[name].dtype))
    for name, factor in factors.items():
        out[name] = (out[name] * factor).astype(out[name].dtype)
    return out
```

```python
from contextlib import ExitStack

import concourse.bass as bass
from concourse import mybir

ALU = mybir.AluOpType
ACT = mybir.ActivationFunctionType
AX_X = mybir.AxisListType.X
F32 = mybir.dt.float32
F16 = mybir.dt.float16
BF16 = mybir.dt.bfloat16
I32 = mybir.dt.int32
U32 = mybir.dt.uint32

P = 128
EPS = 1e-5
SLOPE = 0.2
BIG = 9e15
SAMPLES = 25
HALF = 512
ROOT_SEED = 1597463007.0


def gnn_stack(nc, x, adj, L0_gnn_W, L0_gnn_b, L1_gnn_W, L1_gnn_a, L2_gnn_W, L2_gnn_a,
              L3_gnn_w_rel1, L3_gnn_w_root1, L3_gnn_b1, L3_gnn_w_rel2, L3_gnn_w_root2, L3_gnn_b2, out):
    B, N, C = x.shape
    T = N // P
    ROUNDS = -(-SAMPLES // 8)
    assert C == P and T == 8

    with ExitStack() as ctx:
        def sb(name, shape, dt):
            return ctx.enter_context(nc.sbuf_tensor(name, shape, dt))

        def sem(name):
            return ctx.enter_context(nc.semaphore(name))

        h0_rows = [nc.dram_tensor(f"h0_rows{q}", [N + 1, C], F32, kind="Internal").ap() for q in range(2)]

        ident = sb("ident", [P, P], F32)
        ident_bf = sb("ident_bf", [P, P], BF16)
        ones = sb("ones", [P, P], F32)
        ones_bf = sb("ones_bf", [P, P], BF16)
        zero_row = sb("zero_row", [1, C], F32)
        countdown = sb("countdown", [P, N], F16)
        w0 = sb("w0", [P, 2, C], F32)
        b0_row = sb("b0_row", [1, HALF], F32)
        w1 = sb("w1", [P, C], F32)
        w2 = sb("w2", [P, C], F32)
        w1T = sb("w1T", [P, C], F32)
        w2T = sb("w2T", [P, C], F32)
        att_cols = sb("att_cols", [P, 4], F32)
        att_wide = sb("att_wide", [P, 4, P], F32)
        score_w = sb("score_w", [P, 4, P], F32)
        conv_w = sb("conv_w", [P, 4, C], F32)
        conv_b = sb("conv_b", [P, 2], F32)

        xs = [sb(f"xs{q}", [P, T, C], F32) for q in range(2)]
        kinds = [sb(f"kinds{q}", [P, T, N], BF16) for q in range(2)]
        h0 = [sb(f"h0_{q}", [P, T, C], F32) for q in range(2)]
        agg = [sb(f"agg{q}", [P, T, C], F32) for q in range(2)]

        raw = sb("raw", [P, 3, N], I32)
        key = sb("key", [P, N], F16)
        top = sb("top", [P, 8 * ROUNDS], F16)
        idx = sb("idx", [P, 4, 8 * ROUNDS], U32)
        gath = sb("gath", [P, 2, SAMPLES * C], F32)

        mask = sb("mask", [P, T, N], BF16)
        maskT = sb("maskT", [P, T, N], BF16)
        hn = sb("hn", [P, T, C], F32)
        hT = sb("hT", [P, N], F32)
        aggT = sb("aggT", [P, N], F32)
        gn = sb("gn", [P, T, C], F32)
        rowneg = sb("rowneg", [P, N], F32)
        rowneg02 = sb("rowneg02", [P, N], F32)
        colneg = sb("colneg", [P, T], F32)
        tmp = sb("tmp", [P, N], F32)
        score = sb("score", [P, 2, N], F32)
        prob = sb("prob", [P, 2, N], F32)
        probT = sb("probT", [P, 2, N], F32)
        negmax = sb("negmax", [P, T], F32)
        total = sb("total", [P, T], F32)
        rtotal = sb("rtotal", [P, T], F32)
        gz = sb("gz", [P, 2, C], F32)
        parts = sb("parts", [P, 3, N], BF16)
        ideg = probT[:, 0, :]
        pos = probT[:, 1, :]
        rest = prob[:, 0, :]
        ebuf = prob[:, 1, :]
        hcT = sb("hcT", [P, N], F32)
        stats = sb("stats", [P, T, 6], F32)
        mv = sb("mv", [P, T, 2], F32)
        var = sb("var", [P, T], F32)
        root = sb("root", [P, T], F32)
        sq = sb("sq", [P, T], F32)

        psA, psB, psC, psD = [ctx.enter_context(nc.psum_tensor(n, [P, N], F32)) for n in ("psA", "psB", "psC", "psD")]
        psDb = psD[:, :].bitcast(BF16).rearrange("p (h t i) -> p h t i", h=2, t=T)

        consts_ready = sem("consts_ready")
        weights_in = sem("weights_in")
        wT_ps = sem("wT_ps")
        wT_sb = sem("wT_sb")
        att_wide_ready = sem("att_wide_ready")
        score_w_ps = sem("score_w_ps")
        score_w_sb = sem("score_w_sb")
        zero_stored = sem("zero_stored")
        sp_turn = sem("sp_turn")
        pool_turn = sem("pool_turn")
        x_in = sem("x_in")
        adj_in = [sem(f"adj_in{i}") for i in range(3)]
        raw_used = sem("raw_used")
        h0_ready = sem("h0_ready")
        h0_stored = sem("h0_stored")
        idx_ready = sem("idx_ready")
        gathered = [sem(f"gathered{i}") for i in range(2)]
        reduced = sem("reduced")
        h0T_ps = sem("h0T_ps")
        aggT_ps = sem("aggT_ps")
        hT_sb = sem("hT_sb")
        aggT_sb = sem("aggT_sb")
        lin0_ps = sem("lin0_ps")
        mask_ready = sem("mask_ready")
        maskT_ps = sem("maskT_ps")
        maskT_sb = sem("maskT_sb")
        hn_ready = sem("hn_ready")
        hnT_ps = sem("hnT_ps")
        proj_ps = sem("proj_ps")
        proj_sb = sem("proj_sb")
        score_ready = sem("score_ready")
        prob_sb = sem("prob_sb")
        gz_ready = sem("gz_ready")
        pv_done = sem("pv_done")
        att1_ps = sem("att1_ps")
        elu_arg = sem("elu_arg")
        elu_exp = sem("elu_exp")
        probT_ps = sem("probT_ps")
        probT_sb = sem("probT_sb")
        ctx_done = sem("ctx_done")
        parts_ready = sem("parts_ready")
        deg_ps = sem("deg_ps")
        neigh_ps = sem("neigh_ps")
        neighT_sb = sem("neighT_sb")
        conv_ps = sem("conv_ps")
        hc_ready = sem("hc_ready")
        hc_ps = sem("hc_ps")
        x_final = sem("x_final")
        out_stored = sem("out_stored")
        dve_step = sem("dve_step")

        x_v = x.rearrange("b (t p) c -> b p t c", p=P)
        out_v = out.rearrange("b (t p) c -> b p t c", p=P)
        adj_v = adj.rearrange("b (t p) j -> b t p j", p=P)
        WEIGHT_DMAS = 16

        block = ctx.enter_context(nc.Block())


        @block.sync
        def _(sp):
            def load_x(g, q):
                sp.dma_start(xs[q][:, :, :], x_v[g]).then_inc(x_in, 16)

            def store_h0(g, q):
                sp.wait_ge(h0_ready, g + 1)
                sp.sem_inc(sp_turn, 1)
                sp.dma_start(h0_rows[q][0:N].rearrange("(t p) c -> p t c", p=P), h0[q][:, :, :]).then_inc(h0_stored, 16)

            def adj_tile(g, t, first=False):
                if not first:
                    sp.wait_ge(raw_used, 8 * g + (-1, 0, -2, 1, 2, 3, 4, 5)[t])
                    sp.sem_inc(sp_turn, 1)
                sp.dma_start(raw[:, t % 3, :], adj_v[g, t]).then_inc(adj_in[t % 3], 16)

            load_x(0, 0)
            for t in range(3):
                adj_tile(0, t, first=True)
            for dst, src in (
                (w0[:, 0, :], L0_gnn_W[0:C]), (w0[:, 1, :], L0_gnn_W[C:2 * C]),
                (w1[:, :], L1_gnn_W), (w2[:, :], L2_gnn_W),
                (att_cols[:, 0:1], L1_gnn_a[0:C]), (att_cols[:, 1:2], L1_gnn_a[C:2 * C]),
                (att_cols[:, 2:3], L2_gnn_a[:, C:2 * C].rearrange("a o -> o a")),
                (att_cols[:, 3:4], L2_gnn_a[:, 0:C].rearrange("a o -> o a")),
                (conv_w[:, 0, :], L3_gnn_w_root1), (conv_w[:, 1, :], L3_gnn_w_rel1[1]),
                (conv_w[:, 2, :], L3_gnn_w_root2), (conv_w[:, 3, :], L3_gnn_w_rel2[1]),
                (conv_b[:, 0:1], L3_gnn_b1.rearrange("(o a) -> o a", a=1)),
                (conv_b[:, 1:2], L3_gnn_b2.rearrange("(o a) -> o a", a=1)),
            ):
                sp.dma_start(dst, src).then_inc(weights_in, 16)
            for r in range(HALF // C):
                sp.dma_start(b0_row[0:1, r * C:(r + 1) * C], L0_gnn_b.rearrange("(a o) -> a o", a=1)).then_inc(weights_in, 16)
            sp.wait_ge(consts_ready, 1)
            for q in range(2):
                sp.dma_start(h0_rows[q][N:N + 1, :], zero_row[0:1, :]).then_inc(zero_stored, 16)
            store_h0(0, 0)
            for t in range(3, T):
                adj_tile(0, t)
            load_x(1, 1)
            adj_tile(1, 0)
            adj_tile(1, 1)
            store_h0(1, 1)

            def iteration(g, q, ahead=2):
                if ahead >= 1:
                    for t in range(2, T):
                        adj_tile(g + 1, t)
                sp.wait_ge(x_final, g + 1)
                sp.sem_inc(sp_turn, 1)
                sp.dma_start(out_v[g], xs[q][:, :, :]).then_inc(out_stored, 16)
                if ahead >= 2:
                    sp.wait_ge(out_stored, 16 * g + 16)
                    sp.sem_inc(sp_turn, 1)
                    load_x(g + 2, q)
                    adj_tile(g + 2, 0)
                    adj_tile(g + 2, 1)
                    sp.wait_ge(reduced, 8 * g + 8)
                    sp.sem_inc(sp_turn, 1)
                    store_h0(g + 2, q)

            with sp.Fori(0, (B - 2) // 2) as pair:
                for q in range(2):
                    iteration(pair * 2 + q, q)
            iteration(B - 2, 0, ahead=1)
            iteration(B - 1, 1, ahead=0)
            sp.wait_ge(out_stored, 16 * B)

        @block.gpsimd
        def _(pool):
            nc.gpsimd.memset(zero_row[:, :], 0.0)
            nc.gpsimd.memset(ones[:, :], 1.0)
            nc.gpsimd.memset(ones_bf[:, :], 1.0)
            nc.gpsimd.iota(countdown[:, :], pattern=[[-1, N]], base=N, channel_multiplier=0,
                           allow_small_or_imprecise_dtypes=True)
            nc.gpsimd.memset(ident[:, :], 0.0).then_inc(consts_ready, 1)
            pool.wait_ge(consts_ready, 1)
            nc.gpsimd.affine_select(out=ident[:, :], in_=ident[:, :], compare_op=ALU.not_equal, fill=1.0, base=0,
                                    pattern=[[-1, P]], channel_multiplier=1).then_inc(consts_ready, 1)
            pool.wait_ge(consts_ready, 2)
            nc.gpsimd.tensor_copy(ident_bf[:, :], ident[:, :]).then_inc(consts_ready, 1)
            pool.wait_ge(zero_stored, 32)

            def gather(g, q, first=False):
                pool.wait_ge(h0_stored, 16 * g + 16)
                for t in range(T):
                    pool.wait_ge(idx_ready, 8 * g + t + 1)
                    if not (first and t < 2):
                        pool.wait_ge(reduced, 8 * g + t - 1)
                    pool.sem_inc(pool_turn, 1)
                    for s in range(SAMPLES):
                        nc.gpsimd.indirect_dma_start(
                            out=gath[:, t % 2, s * C:(s + 1) * C], out_offset=None, in_=h0_rows[q][:, :],
                            in_offset=bass.IndirectOffsetOnAxis(ap=idx[:, t % 4, s:s + 1], axis=0),
                        ).then_inc(gathered[t % 2], 16)

            gather(0, 0, first=True)
            with pool.Fori(0, (B - 2) // 2) as pair:
                gather(pair * 2 + 1, 1)
                gather(pair * 2 + 2, 0)
            gather(B - 1, 1)

        @block.scalar
        def _(act):
            act.wait_ge(wT_ps, 1)
            nc.scalar.copy(w1T[:, :], psA[:, 0:P])
            nc.scalar.copy(w2T[:, :], psA[:, P:2 * P]).then_inc(wT_sb, 1)
            act.wait_ge(score_w_ps, 1)
            nc.scalar.copy(score_w[:, :, :].rearrange("p a c -> p (a c)"), psB[:, 0:HALF]).then_inc(score_w_sb, 1)

            def projections(g, layer):
                act.wait_ge(hnT_ps, 3 * g + 1 + layer)
                nc.scalar.activation(hT[:, :], psB[:, :], ACT.Relu).then_inc(hT_sb, 1)
                act.wait_ge(proj_ps, 2 * g + 1 + layer)
                nc.scalar.mul(colneg[:, :], psD[:, 0:T], SLOPE - 1.0)
                nc.scalar.mul(rowneg[:, :], psC[:, :], -1.0)
                nc.scalar.mul(rowneg02[:, :], psC[:, :], -SLOPE)
                nc.scalar.copy(gn[:, :, :].rearrange("p t c -> p (t c)"), psA[:, :]).then_inc(proj_sb, 1)

            def softmax(g, layer, t):
                n = 8 * layer + t
                act.wait_ge(score_ready, 16 * g + n + 1)
                if layer == 0 and t >= 2:
                    act.wait_ge(pv_done, 8 * g + t - 1)
                if layer == 1 and t >= 2:
                    act.wait_ge(probT_ps, 8 * g + t - 1)
                nc.scalar.activation(prob[:, t % 2, :], score[:, t % 2, :], ACT.Exp, bias=negmax[:, t:t + 1],
                                     scale=-1.0, accum_out=total[:, t:t + 1]).then_inc(prob_sb, 1)

            def move_probT(g, t):
                act.wait_ge(probT_ps, 8 * g + t + 1)
                if t >= 2:
                    act.wait_ge(ctx_done, 8 * g + t - 1)
                nc.scalar.copy(probT[:, t % 2, :], (psB, psC)[t % 2][:, :]).then_inc(probT_sb, 1)

            def elu(g, n):
                act.wait_ge(elu_arg, 3 * g + n + 1)
                nc.scalar.activation(ebuf, tmp[:, :], ACT.Exp).then_inc(elu_exp, 1)

            def iteration(g, q):
                act.wait_ge(h0T_ps, g + 1)
                nc.scalar.copy(hT[:, :], psB[:, :]).then_inc(hT_sb, 1)
                act.wait_ge(aggT_ps, g + 1)
                nc.scalar.copy(aggT[:, :], psC[:, :]).then_inc(aggT_sb, 1)
                for t in range(T):
                    act.wait_ge(maskT_ps, 8 * g + t + 1)
                    nc.scalar.copy(maskT[:, :, t * P:(t + 1) * P], psDb[:, t % 2]).then_inc(maskT_sb, 1)
                projections(g, 0)
                for t in range(T):
                    softmax(g, 0, t)
                act.wait_ge(pv_done, 8 * g + T)
                nc.scalar.copy(hT[:, :], psB[:, :]).then_inc(hT_sb, 1)
                elu(g, 0)
                act.wait_ge(gz_ready, 8 * g + T)
                projections(g, 1)
                for t in range(T):
                    softmax(g, 1, t)
                    if t >= 1:
                        move_probT(g, t - 1)
                move_probT(g, T - 1)
                act.wait_ge(hnT_ps, 3 * g + 3)
                nc.scalar.copy(hT[:, :], psB[:, :]).then_inc(hT_sb, 1)
                elu(g, 1)
                elu(g, 2)

            with act.Fori(0, (B - 2) // 2) as pair:
                for q in range(2):
                    iteration(pair * 2 + q, q)
            iteration(B - 2, 0)
            iteration(B - 1, 1)

        @block.vector
        def _(dve):
            chain = {"n": 0}

            def link(ins):
                chain["n"] += 1
                ins.then_inc(dve_step, 1)
                dve.wait_ge(dve_step, chain["n"])

            def restart_links():
                dve.sem_clear(dve_step)
                chain["n"] = 0

            V = nc.vector

            def flat(a):
                return a.rearrange("p t c -> p (t c)")

            def normalise(src, dst, relu):
                for t in range(T):
                    last = V.bn_stats(stats[:, t, :], src[:, t, :])
                link(last)
                for t in range(T):
                    last = V.bn_aggr(mv[:, t, :], stats[:, t, :])
                link(last)
                link(V.tensor_scalar(var[:, :], mv[:, :, 1], EPS, None, ALU.add))
                link(V.tensor_scalar(root[:, :].bitcast(I32), var[:, :].bitcast(I32), -0.5, ROOT_SEED, ALU.mult, ALU.add))
                for _ in range(3):
                    link(V.tensor_tensor(sq[:, :], root[:, :], root[:, :], ALU.mult))
                    link(V.tensor_tensor(sq[:, :], sq[:, :], var[:, :], ALU.mult))
                    link(V.tensor_scalar(sq[:, :], sq[:, :], -0.5, 1.5, ALU.mult, ALU.add))
                    link(V.tensor_tensor(root[:, :], root[:, :], sq[:, :], ALU.mult))
                for t in range(T):
                    last = V.tensor_scalar(dst[:, t, :], src[:, t, :], mv[:, t, 0:1], root[:, t:t + 1], ALU.subtract, ALU.mult)
                if relu:
                    link(last)
                    last = V.tensor_scalar(flat(dst[:, :, :]), flat(dst[:, :, :]), 0.0, None, ALU.max)
                return last

            def select(g, q, t):
                dve.wait_ge(adj_in[t % 3], 16 * ((3 if t % 3 < 2 else 2) * g + t // 3 + 1))
                V.tensor_scalar(kinds[q][:, t, :], raw[:, t % 3, :], -1.0, 2.0, ALU.max, ALU.min)
                link(V.scalar_tensor_tensor(out=key[:, :], in0=raw[:, t % 3, :], scalar=0.0, in1=countdown[:, :],
                                            op0=ALU.not_equal, op1=ALU.mult))
                for r in range(ROUNDS):
                    link(V.max(top[:, 8 * r:8 * r + 8], key[:, :]))
                    if r == 0:
                        dve.sem_inc(raw_used, 1)
                    if r < ROUNDS - 1:
                        link(V.match_replace(key[:, :], top[:, 8 * r:8 * r + 8], key[:, :], 0.0))
                V.tensor_scalar(idx[:, t % 4, :], top[:, :], -1.0, float(N), ALU.mult, ALU.add).then_inc(idx_ready, 1)

            def reduce(g, q, t):
                dve.wait_ge(gathered[t % 2], 16 * SAMPLES * (4 * g + t // 2 + 1))
                V.tensor_reduce(out=agg[q][:, t, :], in_=gath[:, t % 2, :].rearrange("p (s c) -> p c s", c=C),
                                axis=AX_X, op=ALU.max).then_inc(reduced, 1)

            def head(g, q):
                dve.wait_ge(x_in, 16 * g + 16)
                normalise(xs[q], h0[q], True).then_inc(h0_ready, 1)
                select(g, q, 0)
                select(g, q, 1)

            def scores(g, layer, t):
                n = 8 * layer + t
                if n >= 2:
                    dve.wait_ge(prob_sb, 16 * g + n - 1)
                leaky = (tmp, hcT)[t % 2][:, :]
                link(V.scalar_tensor_tensor(out=leaky, in0=rowneg[:, :], scalar=colneg[:, t:t + 1],
                                            in1=rowneg02[:, :], op0=ALU.add, op1=ALU.min))
                V.tensor_tensor_reduce(out=score[:, t % 2, :], in0=leaky, in1=(maskT, mask)[layer][:, t, :],
                                       scale=1.0, scalar=3e38, op0=ALU.add, op1=ALU.min,
                                       accum_out=negmax[:, t:t + 1]).then_inc(score_ready, 1)

            def scale_rows(g, t):
                dve.wait_ge(prob_sb, 16 * g + t + 1)
                link(V.reciprocal(rtotal[:, t:t + 1], total[:, t:t + 1]))
                if t >= 2:
                    dve.wait_ge(pv_done, 8 * g + t - 1)
                V.tensor_scalar(gz[:, t % 2, :], gn[:, t, :], rtotal[:, t:t + 1], None, ALU.mult).then_inc(gz_ready, 1)

            def split(src):
                link(V.tensor_copy(parts[:, 0, :], src))
                link(V.tensor_tensor(rest, src, parts[:, 0, :], ALU.subtract))
                link(V.tensor_copy(parts[:, 1, :], rest))
                link(V.tensor_tensor(rest, rest, parts[:, 1, :], ALU.subtract))
                V.tensor_copy(parts[:, 2, :], rest).then_inc(parts_ready, 1)

            def conv(g, n):
                dve.wait_ge(neigh_ps, 2 * g + n + 1)
                V.tensor_tensor(aggT[:, :], psA[:, :], ideg, ALU.mult).then_inc(neighT_sb, 1)
                dve.wait_ge(conv_ps, 2 * g + n + 1)
                V.tensor_scalar(tmp[:, :], psD[:, :], conv_b[:, n:n + 1], 0.0, ALU.add, ALU.min).then_inc(elu_arg, 1)
                link(V.tensor_scalar(pos, psD[:, :], conv_b[:, n:n + 1], 0.0, ALU.add, ALU.max))
                dve.wait_ge(elu_exp, 3 * g + n + 2)
                V.scalar_tensor_tensor(out=hcT[:, :], in0=ebuf, scalar=-1.0, in1=pos,
                                       op0=ALU.add, op1=ALU.add).then_inc(hc_ready, 1)

            def iteration(g, q, ahead=2):
                o = 1 - q
                restart_links()
                X = flat(xs[q][:, :, :])
                if ahead >= 1:
                    select(g + 1, o, 2)
                V.tensor_scalar(flat(mask[:, :, :]), flat(kinds[q][:, :, :]), 0.0, BIG, ALU.is_le, ALU.mult).then_inc(mask_ready, 1)
                dve.wait_ge(lin0_ps, g + 1)
                link(V.scalar_tensor_tensor(out=X, in0=psA[:, :], scalar=0.0, in1=X, op0=ALU.max, op1=ALU.add))
                normalise(xs[q], hn, False).then_inc(hn_ready, 1)
                if ahead >= 1:
                    reduce(g + 1, o, 0)
                    select(g + 1, o, 3)
                dve.wait_ge(maskT_sb, 8 * g + T)
                dve.wait_ge(proj_sb, 2 * g + 1)
                for t in range(T):
                    scores(g, 0, t)
                    if t >= 1:
                        scale_rows(g, t - 1)
                    if t == T // 2 and ahead >= 1:
                        select(g + 1, o, 4)
                scale_rows(g, T - 1)
                if ahead >= 1:
                    reduce(g + 1, o, 1)
                dve.wait_ge(att1_ps, g + 1)
                V.tensor_scalar(tmp[:, :], psC[:, :], 0.0, None, ALU.min).then_inc(elu_arg, 1)
                link(V.scalar_tensor_tensor(out=X, in0=psC[:, :], scalar=0.0, in1=X, op0=ALU.max, op1=ALU.add))
                dve.wait_ge(elu_exp, 3 * g + 1)
                link(V.scalar_tensor_tensor(out=X, in0=ebuf, scalar=-1.0, in1=X, op0=ALU.add, op1=ALU.add))
                normalise(xs[q], hn, False).then_inc(hn_ready, 1)
                V.tensor_scalar(flat(mask[:, :, :]), flat(kinds[q][:, :, :]), 0.0, BIG, ALU.is_equal, ALU.mult).then_inc(mask_ready, 1)
                if ahead >= 1:
                    select(g + 1, o, 5)
                dve.wait_ge(mask_ready, 3 * g + 2)
                dve.wait_ge(proj_sb, 2 * g + 2)
                for t in range(T):
                    scores(g, 1, t)
                    if t == T // 2 and ahead >= 1:
                        reduce(g + 1, o, 2)
                        select(g + 1, o, 6)
                dve.wait_ge(prob_sb, 16 * g + 16)
                link(V.reciprocal(rtotal[:, :], total[:, :]))
                dve.wait_ge(ctx_done, 8 * g + T)
                for t in range(T):
                    last = V.scalar_tensor_tensor(out=xs[q][:, t, :], in0=psA[:, t * P:(t + 1) * P],
                                                  scalar=rtotal[:, t:t + 1], in1=xs[q][:, t, :], op0=ALU.mult, op1=ALU.add)
                link(last)
                normalise(xs[q], hn, True).then_inc(hn_ready, 1)
                V.tensor_scalar(flat(mask[:, :, :]), flat(kinds[q][:, :, :]), 1.0, None, ALU.is_equal).then_inc(mask_ready, 1)
                dve.wait_ge(hn_ready, 3 * g + 3)
                split(flat(hn[:, :, :]))
                if ahead >= 1:
                    reduce(g + 1, o, 3)
                    select(g + 1, o, 7)
                dve.wait_ge(deg_ps, g + 1)
                link(V.tensor_scalar(ideg, psC[:, :], 1.0, None, ALU.max))
                link(V.reciprocal(ideg, ideg))
                conv(g, 0)
                dve.wait_ge(hc_ps, 2 * g + 1)
                split(psB[:, :])
                if ahead >= 1:
                    reduce(g + 1, o, 4)
                conv(g, 1)
                dve.wait_ge(hc_ps, 2 * g + 2)
                V.tensor_tensor(X, psB[:, :], X, ALU.add).then_inc(x_final, 1)
                if ahead >= 1:
                    reduce(g + 1, o, 5)
                if ahead >= 2:
                    head(g + 2, q)
                if ahead >= 1:
                    reduce(g + 1, o, 6)
                    reduce(g + 1, o, 7)

            dve.wait_ge(consts_ready, 3)
            head(0, 0)
            dve.wait_ge(weights_in, 16 * 18)
            for a in range(4):
                last = V.tensor_scalar(att_wide[:, a, :], ones[:, :], att_cols[:, a:a + 1], None, ALU.mult)
            last.then_inc(att_wide_ready, 1)
            select(0, 0, 2)
            select(0, 0, 3)
            for t in range(6):
                reduce(0, 0, t)
                if t < 4:
                    select(0, 0, t + 4)
            head(1, 1)
            reduce(0, 0, 6)
            reduce(0, 0, 7)
            with dve.Fori(0, (B - 2) // 2) as pair:
                for q in range(2):
                    iteration(pair * 2 + q, q)
            iteration(B - 2, 0, ahead=1)
            iteration(B - 1, 1, ahead=0)

        @block.tensor
        def _(pe):
            def transposes(dst, src, identity):
                for t in range(T):
                    last = nc.tensor.transpose(dst[:, t * P:(t + 1) * P], src[:, t * P:(t + 1) * P], identity)
                return last

            def flat(a):
                return a.rearrange("p t c -> p (t c)")

            pe.wait_ge(weights_in, 16 * 18)
            pe.wait_ge(consts_ready, 3)
            nc.tensor.transpose(psA[:, 0:P], w1[:, :], ident[:, :])
            nc.tensor.transpose(psA[:, P:2 * P], w2[:, :], ident[:, :]).then_inc(wT_ps, 1)
            pe.wait_ge(wT_sb, 1)
            pe.wait_ge(att_wide_ready, 1)
            nc.tensor.matmul(psB[:, 0:2 * P], w1T[:, :], flat(att_wide[:, 0:2, :]), start=True, stop=True)
            nc.tensor.matmul(psB[:, 2 * P:4 * P], w2[:, :], flat(att_wide[:, 2:4, :]), start=True, stop=True).then_inc(score_w_ps, 1)
            pe.wait_ge(score_w_sb, 1)

            def project(g, layer):
                weight = (w1, w2T)[layer]
                pe.wait_ge(hn_ready, 3 * g + 1 + layer)
                transposes(psB, flat(hn[:, :, :]), ident[:, :]).then_inc(hnT_ps, 1)
                pe.wait_ge(hT_sb, 5 * g + (2, 4)[layer])
                for t in range(T):
                    nc.tensor.matmul(psD[:, t:t + 1], hT[:, t * P:(t + 1) * P], score_w[:, 2 * layer + 1, 0:1], start=True, stop=True)
                for h in range(N // HALF):
                    nc.tensor.matmul(psC[:, h * HALF:(h + 1) * HALF], score_w[:, 2 * layer, :], hT[:, h * HALF:(h + 1) * HALF],
                                     start=True, stop=True)
                for t in range(T):
                    last = nc.tensor.matmul(psA[:, t * P:(t + 1) * P], hT[:, t * P:(t + 1) * P], weight[:, :], start=True, stop=True)
                last.then_inc(proj_ps, 1)

            def conv(g, n):
                pe.wait_ge(parts_ready, 2 * g + n + 1)
                for h in range(N // HALF):
                    for k in range(3):
                        for t in range(T):
                            last = nc.tensor.matmul(psA[:, h * HALF:(h + 1) * HALF], parts[:, k, t * P:(t + 1) * P],
                                                    mask[:, t, h * HALF:(h + 1) * HALF],
                                                    start=(k == 0 and t == 0), stop=(k == 2 and t == T - 1))
                last.then_inc(neigh_ps, 1)
                rootT = (hT, hcT)[n]
                pe.wait_ge(neighT_sb, 2 * g + n + 1)
                if n == 0:
                    pe.wait_ge(hT_sb, 5 * g + 5)
                for h in range(N // HALF):
                    cols = slice(h * HALF, (h + 1) * HALF)
                    nc.tensor.matmul(psD[:, cols], conv_w[:, 2 * n, :], rootT[:, cols], start=True, stop=False)
                    last = nc.tensor.matmul(psD[:, cols], conv_w[:, 2 * n + 1, :], aggT[:, cols], start=False, stop=True)
                last.then_inc(conv_ps, 1)
                pe.wait_ge(hc_ready, 2 * g + n + 1)
                transposes(psB, hcT, ident[:, :]).then_inc(hc_ps, 1)

            def attend(g, t):
                pe.wait_ge(probT_sb, 8 * g + t + 1)
                for j in range(T):
                    last = nc.tensor.matmul(psA[:, t * P:(t + 1) * P], probT[:, t % 2, j * P:(j + 1) * P], gn[:, j, :],
                                            start=(j == 0), stop=(j == T - 1))
                last.then_inc(ctx_done, 1)

            def iteration(g, q):
                pe.wait_ge(h0_ready, g + 1)
                pe.wait_ge(reduced, 8 * g + T)
                transposes(psB, flat(h0[q][:, :, :]), ident[:, :]).then_inc(h0T_ps, 1)
                transposes(psC, flat(agg[q][:, :, :]), ident[:, :]).then_inc(aggT_ps, 1)
                pe.wait_ge(hT_sb, 5 * g + 1)
                pe.wait_ge(aggT_sb, g + 1)
                for h in range(N // HALF):
                    nc.tensor.matmul(psA[:, h * HALF:(h + 1) * HALF], ones[0:1, :], b0_row[0:1, :], start=True, stop=False,
                                     skip_group_check=True)
                    for t in range(h * T // 2, (h + 1) * T // 2):
                        rows = slice(t * P, (t + 1) * P)
                        nc.tensor.matmul(psA[:, rows], hT[:, rows], w0[:, 0, :], start=False, stop=False, skip_group_check=True)
                        last = nc.tensor.matmul(psA[:, rows], aggT[:, rows], w0[:, 1, :], start=False, stop=True, skip_group_check=True)
                last.then_inc(lin0_ps, 1)
                pe.wait_ge(mask_ready, 3 * g + 1)
                for t in range(T):
                    if t >= 2:
                        pe.wait_ge(maskT_sb, 8 * g + t - 1)
                    for j in range(T):
                        last = nc.tensor.transpose(psDb[:, t % 2, j], mask[:, t, j * P:(j + 1) * P], ident_bf[:, :])
                    last.then_inc(maskT_ps, 1)
                pe.wait_ge(maskT_sb, 8 * g + T)
                project(g, 0)
                for t in range(T):
                    pe.wait_ge(prob_sb, 16 * g + t + 1)
                    pe.wait_ge(gz_ready, 8 * g + t + 1)
                    for h in range(N // HALF):
                        cols = slice(h * HALF, (h + 1) * HALF)
                        last = nc.tensor.matmul(psB[:, cols], gz[:, t % 2, :], prob[:, t % 2, cols], start=(t == 0), stop=(t == T - 1))
                    last.then_inc(pv_done, 1)
                pe.wait_ge(hT_sb, 5 * g + 3)
                transposes(psC, hT, ident[:, :]).then_inc(att1_ps, 1)
                project(g, 1)
                pe.wait_ge(proj_sb, 2 * g + 2)
                for t in range(T):
                    pe.wait_ge(prob_sb, 16 * g + 8 + t + 1)
                    if t >= 2:
                        pe.wait_ge(probT_sb, 8 * g + t - 1)
                    transposes((psB, psC)[t % 2], prob[:, t % 2, :], ident[:, :]).then_inc(probT_ps, 1)
                    if t >= 1:
                        attend(g, t - 1)
                attend(g, T - 1)
                pe.wait_ge(hn_ready, 3 * g + 3)
                transposes(psB, flat(hn[:, :, :]), ident[:, :]).then_inc(hnT_ps, 1)
                pe.wait_ge(mask_ready, 3 * g + 3)
                for h in range(N // HALF):
                    for t in range(T):
                        last = nc.tensor.matmul(psC[:, h * HALF:(h + 1) * HALF], ones_bf[:, :], mask[:, t, h * HALF:(h + 1) * HALF],
                                                start=(t == 0), stop=(t == T - 1))
                last.then_inc(deg_ps, 1)
                conv(g, 0)
                conv(g, 1)

            with pe.Fori(0, (B - 2) // 2) as pair:
                for q in range(2):
                    iteration(pair * 2 + q, q)
            iteration(B - 2, 0)
            iteration(B - 1, 1)


_INS = ['x', 'adj', 'L0_gnn_W', 'L0_gnn_b', 'L1_gnn_W', 'L1_gnn_a', 'L2_gnn_W', 'L2_gnn_a', 'L3_gnn_w_rel1',
        'L3_gnn_w_root1', 'L3_gnn_b1', 'L3_gnn_w_rel2', 'L3_gnn_w_root2', 'L3_gnn_b2']
_OUTS = [((8, 1024, 128), 'float32')]


def kernel(**inputs):
    import numpy as _np
    import concourse.bacc as _bacc
    from concourse import mybir as _mybir
    from concourse.bass_utils import run_bass_kernel_spmd as _run

    nc = _bacc.Bacc("TRN2", target_bir_lowering=False, num_devices=1)
    arrays, args = {}, []
    for name in _INS:
        a = _np.ascontiguousarray(inputs[name])
        arrays[f"in_{name}_dram"] = a
        args.append(nc.dram_tensor(f"in_{name}_dram", a.shape, _mybir.dt.from_np(a.dtype), kind="ExternalInput").ap())
    for i, (shape, dtype) in enumerate(_OUTS):
        dt = _mybir.dt.from_np(_np.dtype(dtype))
        args.append(nc.dram_tensor(f"out_{i}_dram", shape, dt, kind="ExternalOutput").ap())
    gnn_stack(nc, *args)
    r = _run(nc, [arrays], core_ids=[0])
    return r.results[0]["out_0_dram"]
```

```python
from contextlib import ExitStack

import concourse.bass as bass
from concourse import mybir

ALU = mybir.AluOpType
ACT = mybir.ActivationFunctionType
AX_X = mybir.AxisListType.X
F32 = mybir.dt.float32
F16 = mybir.dt.float16
BF16 = mybir.dt.bfloat16
I32 = mybir.dt.int32
U32 = mybir.dt.uint32

P = 128
EPS = 1e-5
SLOPE = 0.2
BIG = 9e15
SAMPLES = 25
GSLOTS = 3
HALF = 512
ROOT_SEED = 1597463007.0


def gnn_stack(nc, x, adj, L0_gnn_W, L0_gnn_b, L1_gnn_W, L1_gnn_a, L2_gnn_W, L2_gnn_a,
              L3_gnn_w_rel1, L3_gnn_w_root1, L3_gnn_b1, L3_gnn_w_rel2, L3_gnn_w_root2, L3_gnn_b2, out):
    B, N, C = x.shape
    T = N // P
    ROUNDS = -(-SAMPLES // 8)
    assert C == P and T == 8

    with ExitStack() as ctx:
        def sb(name, shape, dt):
            return ctx.enter_context(nc.sbuf_tensor(name, shape, dt))

        def sem(name):
            return ctx.enter_context(nc.semaphore(name))

        h0_rows = [nc.dram_tensor(f"h0_rows{q}", [N + 1, C], F32, kind="Internal").ap() for q in range(2)]

        ident = sb("ident", [P, P], F32)
        ident_bf = sb("ident_bf", [P, P], BF16)
        ones = sb("ones", [P, P], F32)
        ones_bf = sb("ones_bf", [P, P], BF16)
        zero_row = sb("zero_row", [1, C], F32)
        countdown = sb("countdown", [P, N], F16)
        w0 = sb("w0", [P, 2, C], F32)
        b0_row = sb("b0_row", [1, HALF], F32)
        w1 = sb("w1", [P, C], F32)
        w2 = sb("w2", [P, C], F32)
        w1T = sb("w1T", [P, C], F32)
        w2T = sb("w2T", [P, C], F32)
        att_cols = sb("att_cols", [P, 4], F32)
        att_wide = sb("att_wide", [P, 4, P], F32)
        score_w = sb("score_w", [P, 4, P], F32)
        conv_w = sb("conv_w", [P, 4, C], F32)
        conv_b = sb("conv_b", [P, 2], F32)

        xs = [sb(f"xs{q}", [P, T, C], F32) for q in range(2)]
        kinds = [sb(f"kinds{q}", [P, T, N], BF16) for q in range(2)]
        h0 = [sb(f"h0_{q}", [P, T, C], F32) for q in range(2)]
        agg = sb("agg", [P, T, C], F32)

        raw = sb("raw", [P, 2, N], I32)
        key = sb("key", [P, N], F16)
        top = sb("top", [P, 8 * ROUNDS], F16)
        idx = sb("idx", [P, T, 8 * ROUNDS], U32)
        gath = sb("gath", [P, GSLOTS, SAMPLES * C], F32)

        mask = sb("mask", [P, T, N], BF16)
        maskT = sb("maskT", [P, T, N], BF16)
        hn = sb("hn", [P, T, C], F32)
        hT = sb("hT", [P, N], F32)
        aggT = sb("aggT", [P, N], F32)
        gn = sb("gn", [P, T, C], F32)
        rowneg = sb("rowneg", [P, N], F32)
        rowneg02 = sb("rowneg02", [P, N], F32)
        colneg = sb("colneg", [P, T], F32)
        tmp = sb("tmp", [P, N], F32)
        score = sb("score", [P, 2, N], F32)
        prob = sb("prob", [P, 2, N], F32)
        probT = sb("probT", [P, 2, N], F32)
        negmax = sb("negmax", [P, T], F32)
        total = sb("total", [P, T], F32)
        rtotal = sb("rtotal", [P, T], F32)
        gz = sb("gz", [P, 2, C], F32)
        parts = score[:, :, :].bitcast(BF16).rearrange("p a n -> p (a n)")[:, 0:3 * N].rearrange("p (a n) -> p a n", a=3)
        ideg = probT[:, 0, :]
        pos = probT[:, 1, :]
        rest = prob[:, 0, :]
        ebuf = prob[:, 1, :]
        hcT = sb("hcT", [P, N], F32)
        stats = sb("stats", [P, T, 6], F32)
        mv = sb("mv", [P, T, 2], F32)
        var = sb("var", [P, T], F32)
        root = sb("root", [P, 2, T], F32)
        shift = sb("shift", [P, 2, T], F32)
        conv_negb = sb("conv_negb", [P, 2], F32)
        half = sb("half", [P, T], F32)
        sq = sb("sq", [P, T], F32)

        psA, psB, psC, psD = [ctx.enter_context(nc.psum_tensor(n, [P, N], F32)) for n in ("psA", "psB", "psC", "psD")]
        psDb = psD[:, :].bitcast(BF16).rearrange("p (h t i) -> p h t i", h=2, t=T)

        consts_ready = sem("consts_ready")
        weights_in = sem("weights_in")
        wT_ps = sem("wT_ps")
        wT_sb = sem("wT_sb")
        att_wide_ready = sem("att_wide_ready")
        score_w_ps = sem("score_w_ps")
        score_w_sb = sem("score_w_sb")
        zero_stored = sem("zero_stored")
        sp_turn = sem("sp_turn")
        dve_turn = sem("dve_turn")
        pool_turn = sem("pool_turn")
        x_in = sem("x_in")
        adj_in = [sem(f"adj_in{i}") for i in range(2)]
        raw_used = sem("raw_used")
        kinds_sb = sem("kinds_sb")
        x0_in = sem("x0_in")
        norm0_ready = sem("norm0_ready")
        norm_ready = sem("norm_ready")
        h0_ready = sem("h0_ready")
        h0_stored = sem("h0_stored")
        idx_ready = sem("idx_ready")
        gathered = [sem(f"gathered{i}") for i in range(GSLOTS)]
        reduced = sem("reduced")
        h0T_ps = sem("h0T_ps")
        aggT_ps = sem("aggT_ps")
        hT_sb = sem("hT_sb")
        aggT_sb = sem("aggT_sb")
        lin0_ps = sem("lin0_ps")
        mask_ready = sem("mask_ready")
        maskT_ps = sem("maskT_ps")
        maskT_sb = sem("maskT_sb")
        hn_ready = sem("hn_ready")
        hnT_ps = sem("hnT_ps")
        scores_ps = sem("scores_ps")
        scores_sb = sem("scores_sb")
        proj_ps = sem("proj_ps")
        proj_sb = sem("proj_sb")
        score_ready = sem("score_ready")
        prob_sb = sem("prob_sb")
        gz_ready = sem("gz_ready")
        pv_done = sem("pv_done")
        att1_ps = sem("att1_ps")
        elu_arg = sem("elu_arg")
        elu_sb = sem("elu_sb")
        probT_ps = sem("probT_ps")
        probT_sb = sem("probT_sb")
        ctx_done = sem("ctx_done")
        part_sb = sem("part_sb")
        rest_ready = sem("rest_ready")
        deg_ps = sem("deg_ps")
        neigh_ps = sem("neigh_ps")
        neighT_sb = sem("neighT_sb")
        conv_ps = sem("conv_ps")
        hc_ready = sem("hc_ready")
        hc_ps = sem("hc_ps")
        x_final = sem("x_final")
        out_stored = sem("out_stored")
        dve_step = sem("dve_step")

        x_v = x.rearrange("b (t p) c -> b p t c", p=P)
        out_v = out.rearrange("b (t p) c -> b p t c", p=P)
        adj_v = adj.rearrange("b (t p) j -> b t p j", p=P)
        WEIGHT_DMAS = 16

        block = ctx.enter_context(nc.Block())


        @block.sync
        def _(sp):
            def load_x0(g, q):
                sp.dma_start(h0[q][:, :, :], x_v[g]).then_inc(x0_in, 16)

            def load_x(g, q):
                sp.dma_start(xs[q][:, :, :], x_v[g]).then_inc(x_in, 16)

            def store_h0(g, q):
                sp.wait_ge(h0_ready, g + 1)
                sp.sem_inc(sp_turn, 1)
                sp.dma_start(h0_rows[q][0:N].rearrange("(t p) c -> p t c", p=P), h0[q][:, :, :]).then_inc(h0_stored, 16)

            def load_adj(g, t, first=False):
                if not first:
                    sp.wait_ge(raw_used, 8 * g + t - 1)
                    sp.sem_inc(sp_turn, 1)
                    sp.wait_ge(kinds_sb, 8 * g + t - 1)
                    sp.sem_inc(sp_turn, 1)
                sp.dma_start(raw[:, t % 2, :], adj_v[g, t]).then_inc(adj_in[t % 2], 16)

            load_x0(0, 0)
            load_adj(0, 0, first=True)
            load_adj(0, 1, first=True)
            sp.wait_ge(consts_ready, 1)
            for q in range(2):
                sp.dma_start(h0_rows[q][N:N + 1, :], zero_row[0:1, :]).then_inc(zero_stored, 16)
            store_h0(0, 0)
            load_adj(0, 2)
            for dst, src in (
                (w0[:, 0, :], L0_gnn_W[0:C]), (w0[:, 1, :], L0_gnn_W[C:2 * C]),
                (w1[:, :], L1_gnn_W), (w2[:, :], L2_gnn_W),
                (att_cols[:, 0:1], L1_gnn_a[0:C]), (att_cols[:, 1:2], L1_gnn_a[C:2 * C]),
                (att_cols[:, 2:3], L2_gnn_a[:, C:2 * C].rearrange("a o -> o a")),
                (att_cols[:, 3:4], L2_gnn_a[:, 0:C].rearrange("a o -> o a")),
                (conv_w[:, 0, :], L3_gnn_w_root1), (conv_w[:, 1, :], L3_gnn_w_rel1[1]),
                (conv_w[:, 2, :], L3_gnn_w_root2), (conv_w[:, 3, :], L3_gnn_w_rel2[1]),
                (conv_b[:, 0:1], L3_gnn_b1.rearrange("(o a) -> o a", a=1)),
                (conv_b[:, 1:2], L3_gnn_b2.rearrange("(o a) -> o a", a=1)),
            ):
                sp.dma_start(dst, src).then_inc(weights_in, 16)
            for r in range(HALF // C):
                sp.dma_start(b0_row[0:1, r * C:(r + 1) * C], L0_gnn_b.rearrange("(a o) -> a o", a=1)).then_inc(weights_in, 16)
            load_x(0, 0)
            for t in range(3, T):
                load_adj(0, t)
            load_x0(1, 1)
            load_adj(1, 0)
            store_h0(1, 1)
            load_adj(1, 1)
            load_adj(1, 2)
            load_adj(1, 3)
            load_x(1, 1)

            def iteration(g, q, ahead=2):
                if ahead >= 2:
                    sp.wait_ge(h0T_ps, g + 1)
                    sp.sem_inc(sp_turn, 1)
                    load_x0(g + 2, q)
                if ahead >= 1:
                    for t in range(4, T):
                        load_adj(g + 1, t)
                if ahead >= 2:
                    load_adj(g + 2, 0)
                    sp.wait_ge(reduced, 8 * g + 8)
                    sp.sem_inc(sp_turn, 1)
                    store_h0(g + 2, q)
                    load_adj(g + 2, 1)
                    load_adj(g + 2, 2)
                    load_adj(g + 2, 3)
                sp.wait_ge(x_final, g + 1)
                sp.sem_inc(sp_turn, 1)
                sp.dma_start(out_v[g], xs[q][:, :, :]).then_inc(out_stored, 16)
                if ahead >= 2:
                    sp.wait_ge(out_stored, 16 * g + 16)
                    sp.sem_inc(sp_turn, 1)
                    load_x(g + 2, q)

            with sp.Fori(0, (B - 2) // 2) as pair:
                for q in range(2):
                    iteration(pair * 2 + q, q)
            iteration(B - 2, 0, ahead=1)
            iteration(B - 1, 1, ahead=0)
            sp.wait_ge(out_stored, 16 * B)

        @block.gpsimd
        def _(pool):
            nc.gpsimd.memset(zero_row[:, :], 0.0)
            nc.gpsimd.memset(ones[:, :], 1.0)
            nc.gpsimd.memset(ones_bf[:, :], 1.0)
            nc.gpsimd.iota(countdown[:, :], pattern=[[-1, N]], base=N, channel_multiplier=0,
                           allow_small_or_imprecise_dtypes=True)
            nc.gpsimd.memset(ident[:, :], 0.0).then_inc(consts_ready, 1)
            pool.wait_ge(consts_ready, 1)
            nc.gpsimd.affine_select(out=ident[:, :], in_=ident[:, :], compare_op=ALU.not_equal, fill=1.0, base=0,
                                    pattern=[[-1, P]], channel_multiplier=1).then_inc(consts_ready, 1)
            pool.wait_ge(consts_ready, 2)
            nc.gpsimd.tensor_copy(ident_bf[:, :], ident[:, :]).then_inc(consts_ready, 1)
            pool.wait_ge(zero_stored, 32)

            def gather(g, q, first=False):
                pool.wait_ge(h0_stored, 16 * g + 16)
                for t in range(T):
                    pool.wait_ge(idx_ready, 8 * g + t + 1)
                    if not (first and t < GSLOTS):
                        pool.wait_ge(reduced, 8 * g + (-1, 0, -2, 1, 2, 3, 4, 5)[t])
                    pool.sem_inc(pool_turn, 1)
                    for s in range(SAMPLES):
                        nc.gpsimd.indirect_dma_start(
                            out=gath[:, t % GSLOTS, s * C:(s + 1) * C], out_offset=None, in_=h0_rows[q][:, :],
                            in_offset=bass.IndirectOffsetOnAxis(ap=idx[:, t, s:s + 1], axis=0),
                        ).then_inc(gathered[t % GSLOTS], 16)

            gather(0, 0, first=True)
            with pool.Fori(0, (B - 2) // 2) as pair:
                gather(pair * 2 + 1, 1)
                gather(pair * 2 + 2, 0)
            gather(B - 1, 1)

        @block.scalar
        def _(act):
            def projections(g, layer):
                act.wait_ge(hnT_ps, 3 * g + 1 + layer)
                nc.scalar.activation(hT[:, :], psB[:, :], ACT.Relu).then_inc(hT_sb, 1)
                act.wait_ge(scores_ps, 2 * g + 1 + layer)
                nc.scalar.mul(colneg[:, :], psD[:, 0:T], SLOPE - 1.0)
                nc.scalar.mul(rowneg[:, :], psC[:, :], -1.0)
                nc.scalar.mul(rowneg02[:, :], psC[:, :], -SLOPE).then_inc(scores_sb, 1)
                act.wait_ge(proj_ps, 2 * g + 1 + layer)
                nc.scalar.copy(gn[:, :, :].rearrange("p t c -> p (t c)"), psA[:, :]).then_inc(proj_sb, 1)

            def softmax(g, layer, t):
                n = 8 * layer + t
                act.wait_ge(score_ready, 16 * g + n + 1)
                if layer == 0 and t >= 2:
                    act.wait_ge(pv_done, 8 * g + t - 1)
                if layer == 1 and t >= 2:
                    act.wait_ge(probT_ps, 8 * g + t - 1)
                nc.scalar.activation(prob[:, t % 2, :], score[:, t % 2, :], ACT.Exp, bias=negmax[:, t:t + 1],
                                     scale=-1.0, accum_out=total[:, t:t + 1]).then_inc(prob_sb, 1)

            def move_probT(g, t):
                act.wait_ge(probT_ps, 8 * g + t + 1)
                if t >= 2:
                    act.wait_ge(ctx_done, 8 * g + t - 1)
                nc.scalar.copy(probT[:, t % 2, :], (psB, psC)[t % 2][:, :]).then_inc(probT_sb, 1)

            def copy_kinds(g, q, t):
                act.wait_ge(adj_in[t % 2], 16 * (4 * g + t // 2 + 1))
                nc.scalar.copy(kinds[q][:, t, :], raw[:, t % 2, :]).then_inc(kinds_sb, 1)

            def normalise(src, dst, which, func):
                for t in range(T):
                    last = nc.scalar.activation(dst[:, t, :], src[:, t, :], func, bias=shift[:, which, t:t + 1],
                                                scale=root[:, which, t:t + 1])
                return last

            def normalise0(g, q):
                act.wait_ge(norm0_ready, g + 1)
                normalise(h0[q], h0[q], 1, ACT.Relu).then_inc(h0_ready, 1)

            def normalise_x(g, q, layer):
                act.wait_ge(norm_ready, 3 * g + layer)
                normalise(xs[q], hn, 0, ACT.Relu if layer == 3 else ACT.Identity).then_inc(hn_ready, 1)

            def elu(g, n):
                src = psC if n == 0 else psD
                act.wait_ge(att1_ps if n == 0 else conv_ps, g + 1 if n == 0 else 2 * g + n)
                nc.scalar.activation(ebuf, src[:, :], ACT.Relu, scale=-1.0,
                                     bias=0.0 if n == 0 else conv_negb[:, n - 1:n]).then_inc(elu_arg, 1)
                if n > 0:
                    nc.scalar.activation(pos, src[:, :], ACT.Relu, bias=conv_b[:, n - 1:n])
                act.wait_ge(elu_arg, 3 * g + n + 1)
                nc.scalar.activation(ebuf, ebuf, ACT.Exp, scale=-1.0).then_inc(elu_sb, 1)

            def split(g, n, src):
                nc.scalar.copy(parts[:, 0, :], src).then_inc(part_sb, 1)
                for k in range(1, 3):
                    act.wait_ge(rest_ready, 4 * g + 2 * n + k)
                    nc.scalar.copy(parts[:, k, :], (rest, tmp[:, :])[k - 1]).then_inc(part_sb, 1)

            def iteration(g, q, ahead=2):
                o = 1 - q
                act.wait_ge(h0T_ps, g + 1)
                nc.scalar.copy(hT[:, :], psB[:, :]).then_inc(hT_sb, 1)
                act.wait_ge(aggT_ps, g + 1)
                nc.scalar.copy(aggT[:, :], psC[:, :]).then_inc(aggT_sb, 1)
                if ahead >= 1:
                    copy_kinds(g + 1, o, 3)
                for t in range(T):
                    act.wait_ge(maskT_ps, 8 * g + t + 1)
                    nc.scalar.copy(maskT[:, :, t * P:(t + 1) * P], psDb[:, t % 2]).then_inc(maskT_sb, 1)
                normalise_x(g, q, 1)
                if ahead >= 1:
                    copy_kinds(g + 1, o, 4)
                projections(g, 0)
                if ahead >= 1:
                    copy_kinds(g + 1, o, 5)
                for t in range(T):
                    softmax(g, 0, t)
                act.wait_ge(pv_done, 8 * g + T)
                nc.scalar.copy(hT[:, :], psB[:, :]).then_inc(hT_sb, 1)
                elu(g, 0)
                normalise_x(g, q, 2)
                if ahead >= 1:
                    copy_kinds(g + 1, o, 6)
                projections(g, 1)
                if ahead >= 1:
                    copy_kinds(g + 1, o, 7)
                for t in range(T):
                    softmax(g, 1, t)
                    if t >= 1:
                        move_probT(g, t - 1)
                move_probT(g, T - 1)
                normalise_x(g, q, 3)
                act.wait_ge(hn_ready, 3 * g + 3)
                split(g, 0, hn[:, :, :].rearrange("p t c -> p (t c)"))
                act.wait_ge(hnT_ps, 3 * g + 3)
                nc.scalar.copy(hT[:, :], psB[:, :]).then_inc(hT_sb, 1)
                if ahead >= 2:
                    normalise0(g + 2, q)
                    act.wait_ge(mask_ready, 3 * g + 3)
                    copy_kinds(g + 2, q, 0)
                elu(g, 1)
                act.wait_ge(hc_ps, 2 * g + 1)
                split(g, 1, psB[:, :])
                if ahead >= 2:
                    copy_kinds(g + 2, q, 1)
                    copy_kinds(g + 2, q, 2)
                elu(g, 2)

            copy_kinds(0, 0, 0)
            normalise0(0, 0)
            for t in range(1, T):
                copy_kinds(0, 0, t)
            act.wait_ge(wT_ps, 1)
            nc.scalar.copy(w1T[:, :], psA[:, 0:P])
            nc.scalar.copy(w2T[:, :], psA[:, P:2 * P]).then_inc(wT_sb, 1)
            act.wait_ge(score_w_ps, 1)
            nc.scalar.copy(score_w[:, :, :].rearrange("p a c -> p (a c)"), psB[:, 0:HALF]).then_inc(score_w_sb, 1)
            nc.scalar.mul(conv_negb[:, :], conv_b[:, :], -1.0)
            normalise0(1, 1)
            for t in range(3):
                copy_kinds(1, 1, t)
            with act.Fori(0, (B - 2) // 2) as pair:
                for q in range(2):
                    iteration(pair * 2 + q, q)
            iteration(B - 2, 0, ahead=1)
            iteration(B - 1, 1, ahead=0)

        @block.vector
        def _(dve):
            chain = {"n": 0}

            def step(ins):
                chain["n"] += 1
                ins.then_inc(dve_step, 1)
                return chain["n"]

            def link(ins):
                dve.wait_ge(dve_step, step(ins))

            def restart_links():
                dve.sem_clear(dve_step)
                chain["n"] = 0

            V = nc.vector

            def flat(a):
                return a.rearrange("p t c -> p (t c)")

            def moments(src, which):
                y, m = root[:, which, :], shift[:, which, :]
                for t in range(T):
                    last = V.bn_stats(stats[:, t, :], src[:, t, :])
                link(last)
                for t in range(T):
                    last = V.bn_aggr(mv[:, t, :], stats[:, t, :])
                link(last)
                link(V.tensor_scalar(var[:, :], mv[:, :, 1], EPS, None, ALU.add))
                V.tensor_scalar(y.bitcast(I32), var[:, :].bitcast(I32), -0.5, ROOT_SEED, ALU.mult, ALU.add)
                link(V.tensor_scalar(half[:, :], var[:, :], -0.5, None, ALU.mult))
                for _ in range(3):
                    link(V.tensor_tensor(sq[:, :], y, y, ALU.mult))
                    link(V.tensor_tensor(sq[:, :], sq[:, :], half[:, :], ALU.mult))
                    link(V.scalar_tensor_tensor(out=y, in0=sq[:, :], scalar=1.5, in1=y, op0=ALU.add, op1=ALU.mult))
                return V.scalar_tensor_tensor(out=m, in0=mv[:, :, 0], scalar=-1.0, in1=y, op0=ALU.mult, op1=ALU.mult)

            last_pass = {}

            def select_key(g, t):
                dve.wait_ge(adj_in[t % 2], 16 * (4 * g + t // 2 + 1))
                last_pass["n"] = step(V.scalar_tensor_tensor(out=key[:, :], in0=raw[:, t % 2, :], scalar=0.0, in1=countdown[:, :],
                                                             op0=ALU.not_equal, op1=ALU.mult))

            def select_max(r):
                dve.wait_ge(dve_step, last_pass["n"])
                if r == 0:
                    dve.sem_inc(raw_used, 1)
                last_pass["n"] = step(V.max(top[:, 8 * r:8 * r + 8], key[:, :]))

            def select_drop(r):
                dve.wait_ge(dve_step, last_pass["n"])
                last_pass["n"] = step(V.match_replace(key[:, :], top[:, 8 * r:8 * r + 8], key[:, :], 0.0))

            def select_indices(t):
                dve.wait_ge(dve_step, last_pass["n"])
                V.tensor_scalar(idx[:, t, :], top[:, :], -1.0, float(N), ALU.mult, ALU.add).then_inc(idx_ready, 1)

            def select(g, t):
                select_key(g, t)
                for r in range(ROUNDS):
                    select_max(r)
                    if r < ROUNDS - 1:
                        select_drop(r)
                select_indices(t)

            def reduce(g, t):
                slot = t % GSLOTS
                dve.wait_ge(gathered[slot], 16 * SAMPLES * ((3, 3, 2)[slot] * g + t // GSLOTS + 1))
                V.tensor_reduce(out=agg[:, t, :], in_=gath[:, slot, :].rearrange("p (s c) -> p c s", c=C),
                                axis=AX_X, op=ALU.max).then_inc(reduced, 1)

            def head(g, q):
                dve.wait_ge(x0_in, 16 * g + 16)
                moments(h0[q], 1).then_inc(norm0_ready, 1)

            def leaky(g, layer, t):
                if t >= 2:
                    dve.wait_ge(score_ready, 16 * g + 8 * layer + t - 1)
                return step(V.scalar_tensor_tensor(out=(tmp, hcT)[t % 2][:, :], in0=rowneg[:, :], scalar=colneg[:, t:t + 1],
                                                   in1=rowneg02[:, :], op0=ALU.add, op1=ALU.min))

            def masked(g, layer, t, made):
                n = 8 * layer + t
                if n >= 2:
                    dve.wait_ge(prob_sb, 16 * g + n - 1)
                    dve.sem_inc(dve_turn, 1)
                dve.wait_ge(dve_step, made)
                V.tensor_tensor_reduce(out=score[:, t % 2, :], in0=(tmp, hcT)[t % 2][:, :], in1=(maskT, mask)[layer][:, t, :],
                                       scale=1.0, scalar=3e38, op0=ALU.add, op1=ALU.min,
                                       accum_out=negmax[:, t:t + 1]).then_inc(score_ready, 1)

            def attention(g, layer, ahead, t_ahead):
                if ahead:
                    select_key(g + 1, t_ahead)
                made = leaky(g, layer, 0)
                for t in range(T):
                    after = leaky(g, layer, t + 1) if t + 1 < T else None
                    masked(g, layer, t, made)
                    made = after
                    if layer == 0 and t >= 1:
                        inverse = invert_sum(g, t - 1)
                    if ahead:
                        if t == T - 1:
                            select_indices(t_ahead)
                        elif t % 2 == 0:
                            select_max(t // 2)
                        else:
                            select_drop(t // 2)
                    if layer == 0 and t >= 1:
                        scale_rows(g, t - 1, inverse)
                if layer == 0:
                    scale_rows(g, T - 1, invert_sum(g, T - 1))

            def invert_sum(g, t):
                dve.wait_ge(prob_sb, 16 * g + t + 1)
                return step(V.reciprocal(rtotal[:, t:t + 1], total[:, t:t + 1]))

            def scale_rows(g, t, inverse):
                if t >= 2:
                    dve.wait_ge(pv_done, 8 * g + t - 1)
                if t == 0:
                    dve.wait_ge(proj_sb, 2 * g + 1)
                dve.wait_ge(dve_step, inverse)
                V.tensor_scalar(gz[:, t % 2, :], gn[:, t, :], rtotal[:, t:t + 1], None, ALU.mult).then_inc(gz_ready, 1)

            def split(g, n, src):
                dve.wait_ge(part_sb, 6 * g + 3 * n + 1)
                V.tensor_tensor(rest, src, parts[:, 0, :], ALU.subtract).then_inc(rest_ready, 1)
                dve.wait_ge(part_sb, 6 * g + 3 * n + 2)
                V.tensor_tensor(tmp[:, :], rest, parts[:, 1, :], ALU.subtract).then_inc(rest_ready, 1)

            def divide(g, n):
                dve.wait_ge(neigh_ps, 2 * g + n + 1)
                V.tensor_tensor(aggT[:, :], psA[:, :], ideg, ALU.mult).then_inc(neighT_sb, 1)

            def elu(g, n):
                dve.wait_ge(elu_sb, 3 * g + n + 2)
                V.scalar_tensor_tensor(out=hcT[:, :], in0=ebuf, scalar=-1.0, in1=pos,
                                       op0=ALU.add, op1=ALU.add).then_inc(hc_ready, 1)

            def iteration(g, q, ahead=2):
                X = flat(xs[q][:, :, :])
                restart_links()
                V.tensor_scalar(flat(mask[:, :, :]), flat(kinds[q][:, :, :]), 0.0, BIG, ALU.is_le, ALU.mult).then_inc(mask_ready, 1)
                if ahead >= 1:
                    select(g + 1, 3)
                dve.wait_ge(x_in, 16 * g + 16)
                dve.wait_ge(lin0_ps, g + 1)
                link(V.scalar_tensor_tensor(out=X, in0=psA[:, :], scalar=0.0, in1=X, op0=ALU.max, op1=ALU.add))
                moments(xs[q], 0).then_inc(norm_ready, 1)
                if ahead >= 1:
                    reduce(g + 1, 0)
                    select(g + 1, 4)
                dve.wait_ge(maskT_sb, 8 * g + T)
                dve.wait_ge(scores_sb, 2 * g + 1)
                attention(g, 0, ahead >= 1, 5)
                if ahead >= 1:
                    reduce(g + 1, 1)
                    reduce(g + 1, 2)
                dve.wait_ge(elu_arg, 3 * g + 1)
                link(V.scalar_tensor_tensor(out=X, in0=psC[:, :], scalar=0.0, in1=X, op0=ALU.max, op1=ALU.add))
                dve.wait_ge(elu_sb, 3 * g + 1)
                link(V.scalar_tensor_tensor(out=X, in0=ebuf, scalar=-1.0, in1=X, op0=ALU.add, op1=ALU.add))
                moments(xs[q], 0).then_inc(norm_ready, 1)
                V.tensor_scalar(flat(mask[:, :, :]), flat(kinds[q][:, :, :]), 0.0, BIG, ALU.is_equal, ALU.mult).then_inc(mask_ready, 1)
                if ahead >= 1:
                    select(g + 1, 6)
                    reduce(g + 1, 3)
                dve.wait_ge(mask_ready, 3 * g + 2)
                dve.wait_ge(scores_sb, 2 * g + 2)
                attention(g, 1, ahead >= 1, 7)
                if ahead >= 1:
                    reduce(g + 1, 4)
                dve.wait_ge(prob_sb, 16 * g + 16)
                link(V.reciprocal(rtotal[:, :], total[:, :]))
                dve.wait_ge(ctx_done, 8 * g + T)
                for t in range(T):
                    last = V.scalar_tensor_tensor(out=xs[q][:, t, :], in0=psA[:, t * P:(t + 1) * P],
                                                  scalar=rtotal[:, t:t + 1], in1=xs[q][:, t, :], op0=ALU.mult, op1=ALU.add)
                link(last)
                moments(xs[q], 0).then_inc(norm_ready, 1)
                V.tensor_scalar(flat(mask[:, :, :]), flat(kinds[q][:, :, :]), 1.0, None, ALU.is_equal).then_inc(mask_ready, 1)
                if ahead >= 2:
                    head(g + 2, q)
                split(g, 0, flat(hn[:, :, :]))
                dve.wait_ge(deg_ps, g + 1)
                link(V.tensor_scalar(ideg, psC[:, :], 1.0, None, ALU.max))
                link(V.reciprocal(ideg, ideg))
                if ahead >= 1:
                    reduce(g + 1, 5)
                    reduce(g + 1, 6)
                divide(g, 0)
                if ahead >= 2:
                    select(g + 2, 0)
                elu(g, 0)
                dve.wait_ge(hc_ps, 2 * g + 1)
                split(g, 1, psB[:, :])
                if ahead >= 2:
                    select(g + 2, 1)
                divide(g, 1)
                if ahead >= 2:
                    select(g + 2, 2)
                elu(g, 1)
                dve.wait_ge(hc_ps, 2 * g + 2)
                V.tensor_tensor(X, psB[:, :], X, ALU.add).then_inc(x_final, 1)
                if ahead >= 1:
                    reduce(g + 1, 7)

            dve.wait_ge(consts_ready, 3)
            head(0, 0)
            select(0, 0)
            select(0, 1)
            dve.wait_ge(weights_in, 16 * 18)
            for a in range(4):
                last = V.tensor_scalar(att_wide[:, a, :], ones[:, :], att_cols[:, a:a + 1], None, ALU.mult)
            last.then_inc(att_wide_ready, 1)
            for t in range(2, T):
                select(0, t)
                if t >= 3:
                    reduce(0, t - 3)
            head(1, 1)
            select(1, 0)
            reduce(0, 5)
            select(1, 1)
            reduce(0, 6)
            select(1, 2)
            reduce(0, 7)
            with dve.Fori(0, (B - 2) // 2) as pair:
                for q in range(2):
                    iteration(pair * 2 + q, q)
            iteration(B - 2, 0, ahead=1)
            iteration(B - 1, 1, ahead=0)

        @block.tensor
        def _(pe):
            def transposes(dst, src, identity):
                for t in range(T):
                    last = nc.tensor.transpose(dst[:, t * P:(t + 1) * P], src[:, t * P:(t + 1) * P], identity)
                return last

            def flat(a):
                return a.rearrange("p t c -> p (t c)")

            pe.wait_ge(weights_in, 16 * 18)
            pe.wait_ge(consts_ready, 3)
            nc.tensor.transpose(psA[:, 0:P], w1[:, :], ident[:, :])
            nc.tensor.transpose(psA[:, P:2 * P], w2[:, :], ident[:, :]).then_inc(wT_ps, 1)
            pe.wait_ge(wT_sb, 1)
            pe.wait_ge(att_wide_ready, 1)
            nc.tensor.matmul(psB[:, 0:2 * P], w1T[:, :], flat(att_wide[:, 0:2, :]), start=True, stop=True)
            nc.tensor.matmul(psB[:, 2 * P:4 * P], w2[:, :], flat(att_wide[:, 2:4, :]), start=True, stop=True).then_inc(score_w_ps, 1)
            pe.wait_ge(score_w_sb, 1)

            def project(g, layer):
                weight = (w1, w2T)[layer]
                pe.wait_ge(hn_ready, 3 * g + 1 + layer)
                transposes(psB, flat(hn[:, :, :]), ident[:, :]).then_inc(hnT_ps, 1)
                pe.wait_ge(hT_sb, 5 * g + (2, 4)[layer])
                for t in range(T):
                    nc.tensor.matmul(psD[:, t:t + 1], hT[:, t * P:(t + 1) * P], score_w[:, 2 * layer + 1, 0:1], start=True, stop=True)
                for h in range(N // HALF):
                    last = nc.tensor.matmul(psC[:, h * HALF:(h + 1) * HALF], score_w[:, 2 * layer, :],
                                            hT[:, h * HALF:(h + 1) * HALF], start=True, stop=True)
                last.then_inc(scores_ps, 1)
                for t in range(T):
                    last = nc.tensor.matmul(psA[:, t * P:(t + 1) * P], hT[:, t * P:(t + 1) * P], weight[:, :], start=True, stop=True)
                last.then_inc(proj_ps, 1)

            def conv(g, n):
                pe.wait_ge(part_sb, 6 * g + 3 * n + 3)
                for h in range(N // HALF):
                    for k in range(3):
                        for t in range(T):
                            last = nc.tensor.matmul(psA[:, h * HALF:(h + 1) * HALF], parts[:, k, t * P:(t + 1) * P],
                                                    mask[:, t, h * HALF:(h + 1) * HALF],
                                                    start=(k == 0 and t == 0), stop=(k == 2 and t == T - 1))
                last.then_inc(neigh_ps, 1)
                rootT = (hT, hcT)[n]
                pe.wait_ge(neighT_sb, 2 * g + n + 1)
                if n == 0:
                    pe.wait_ge(hT_sb, 5 * g + 5)
                for h in range(N // HALF):
                    cols = slice(h * HALF, (h + 1) * HALF)
                    nc.tensor.matmul(psD[:, cols], conv_w[:, 2 * n, :], rootT[:, cols], start=True, stop=False)
                    last = nc.tensor.matmul(psD[:, cols], conv_w[:, 2 * n + 1, :], aggT[:, cols], start=False, stop=True)
                last.then_inc(conv_ps, 1)
                pe.wait_ge(hc_ready, 2 * g + n + 1)
                transposes(psB, hcT, ident[:, :]).then_inc(hc_ps, 1)

            def attend(g, t):
                pe.wait_ge(probT_sb, 8 * g + t + 1)
                for j in range(T):
                    last = nc.tensor.matmul(psA[:, t * P:(t + 1) * P], probT[:, t % 2, j * P:(j + 1) * P], gn[:, j, :],
                                            start=(j == 0), stop=(j == T - 1))
                last.then_inc(ctx_done, 1)

            def iteration(g, q):
                pe.wait_ge(h0_ready, g + 1)
                pe.wait_ge(reduced, 8 * g + T)
                transposes(psB, flat(h0[q][:, :, :]), ident[:, :]).then_inc(h0T_ps, 1)
                transposes(psC, flat(agg[:, :, :]), ident[:, :]).then_inc(aggT_ps, 1)
                pe.wait_ge(hT_sb, 5 * g + 1)
                pe.wait_ge(aggT_sb, g + 1)
                for h in range(N // HALF):
                    nc.tensor.matmul(psA[:, h * HALF:(h + 1) * HALF], ones[0:1, :], b0_row[0:1, :], start=True, stop=False,
                                     skip_group_check=True)
                    for t in range(h * T // 2, (h + 1) * T // 2):
                        rows = slice(t * P, (t + 1) * P)
                        nc.tensor.matmul(psA[:, rows], hT[:, rows], w0[:, 0, :], start=False, stop=False, skip_group_check=True)
                        last = nc.tensor.matmul(psA[:, rows], aggT[:, rows], w0[:, 1, :], start=False, stop=True, skip_group_check=True)
                last.then_inc(lin0_ps, 1)
                pe.wait_ge(mask_ready, 3 * g + 1)
                for t in range(T):
                    if t >= 2:
                        pe.wait_ge(maskT_sb, 8 * g + t - 1)
                    for j in range(T):
                        last = nc.tensor.transpose(psDb[:, t % 2, j], mask[:, t, j * P:(j + 1) * P], ident_bf[:, :])
                    last.then_inc(maskT_ps, 1)
                pe.wait_ge(maskT_sb, 8 * g + T)
                project(g, 0)
                for t in range(T):
                    pe.wait_ge(prob_sb, 16 * g + t + 1)
                    pe.wait_ge(gz_ready, 8 * g + t + 1)
                    for h in range(N // HALF):
                        cols = slice(h * HALF, (h + 1) * HALF)
                        last = nc.tensor.matmul(psB[:, cols], gz[:, t % 2, :], prob[:, t % 2, cols], start=(t == 0), stop=(t == T - 1))
                    last.then_inc(pv_done, 1)
                pe.wait_ge(hT_sb, 5 * g + 3)
                transposes(psC, hT, ident[:, :]).then_inc(att1_ps, 1)
                project(g, 1)
                pe.wait_ge(proj_sb, 2 * g + 2)
                for t in range(T):
                    pe.wait_ge(prob_sb, 16 * g + 8 + t + 1)
                    if t >= 2:
                        pe.wait_ge(probT_sb, 8 * g + t - 1)
                    transposes((psB, psC)[t % 2], prob[:, t % 2, :], ident[:, :]).then_inc(probT_ps, 1)
                    if t >= 1:
                        attend(g, t - 1)
                attend(g, T - 1)
                pe.wait_ge(hn_ready, 3 * g + 3)
                transposes(psB, flat(hn[:, :, :]), ident[:, :]).then_inc(hnT_ps, 1)
                pe.wait_ge(mask_ready, 3 * g + 3)
                for h in range(N // HALF):
                    for t in range(T):
                        last = nc.tensor.matmul(psC[:, h * HALF:(h + 1) * HALF], ones_bf[:, :], mask[:, t, h * HALF:(h + 1) * HALF],
                                                start=(t == 0), stop=(t == T - 1))
                last.then_inc(deg_ps, 1)
                conv(g, 0)
                conv(g, 1)

            with pe.Fori(0, (B - 2) // 2) as pair:
                for q in range(2):
                    iteration(pair * 2 + q, q)
            iteration(B - 2, 0)
            iteration(B - 1, 1)


_INS = ['x', 'adj', 'L0_gnn_W', 'L0_gnn_b', 'L1_gnn_W', 'L1_gnn_a', 'L2_gnn_W', 'L2_gnn_a', 'L3_gnn_w_rel1',
        'L3_gnn_w_root1', 'L3_gnn_b1', 'L3_gnn_w_rel2', 'L3_gnn_w_root2', 'L3_gnn_b2']
_OUTS = [((8, 1024, 128), 'float32')]


def kernel(**inputs):
    import numpy as _np
    import concourse.bacc as _bacc
    from concourse import mybir as _mybir
    from concourse.bass_utils import run_bass_kernel_spmd as _run

    nc = _bacc.Bacc("TRN2", target_bir_lowering=False, num_devices=1)
    arrays, args = {}, []
    for name in _INS:
        a = _np.ascontiguousarray(inputs[name])
        arrays[f"in_{name}_dram"] = a
        args.append(nc.dram_tensor(f"in_{name}_dram", a.shape, _mybir.dt.from_np(a.dtype), kind="ExternalInput").ap())
    for i, (shape, dtype) in enumerate(_OUTS):
        dt = _mybir.dt.from_np(_np.dtype(dtype))
        args.append(nc.dram_tensor(f"out_{i}_dram", shape, dt, kind="ExternalOutput").ap())
    gnn_stack(nc, *args)
    r = _run(nc, [arrays], core_ids=[0])
    return r.results[0]["out_0_dram"]
```

```python
from contextlib import ExitStack

import concourse.bass as bass
from concourse import mybir

ALU = mybir.AluOpType
ACT = mybir.ActivationFunctionType
AX_X = mybir.AxisListType.X
F32 = mybir.dt.float32
F16 = mybir.dt.float16
BF16 = mybir.dt.bfloat16
I32 = mybir.dt.int32
U32 = mybir.dt.uint32

P = 128
EPS = 1e-5
SLOPE = 0.2
BIG = 9e15
SAMPLES = 25
GSLOTS = 3
ALWAYS = 13
PAIRS = (SAMPLES - ALWAYS) // 2
HALF = 512
ROOT_SEED = 1597463007.0


def gnn_stack(nc, x, adj, L0_gnn_W, L0_gnn_b, L1_gnn_W, L1_gnn_a, L2_gnn_W, L2_gnn_a,
              L3_gnn_w_rel1, L3_gnn_w_root1, L3_gnn_b1, L3_gnn_w_rel2, L3_gnn_w_root2, L3_gnn_b2, out):
    B, N, C = x.shape
    T = N // P
    ROUNDS = -(-SAMPLES // 8)
    assert C == P and T == 8

    with ExitStack() as ctx:
        def sb(name, shape, dt):
            return ctx.enter_context(nc.sbuf_tensor(name, shape, dt))

        def sem(name):
            return ctx.enter_context(nc.semaphore(name))

        h0_rows = [nc.dram_tensor(f"h0_rows{q}", [N + 1, C], F32, kind="Internal").ap() for q in range(2)]

        blank = nc.dram_tensor("blank", [P, 2 * PAIRS * C], F32, kind="Internal").ap()

        ident = sb("ident", [P, P], F32)
        ident_bf = sb("ident_bf", [P, P], BF16)
        ones = sb("ones", [P, P], F32)
        ones_bf = sb("ones_bf", [P, P], BF16)
        zero_row = sb("zero_row", [1, C], F32)
        countdown = sb("countdown", [P, N], F16)
        w0 = sb("w0", [P, 2, C], F32)
        b0_row = sb("b0_row", [1, HALF], F32)
        w1 = sb("w1", [P, C], F32)
        w2 = sb("w2", [P, C], F32)
        w1T = sb("w1T", [P, C], F32)
        w2T = sb("w2T", [P, C], F32)
        att_cols = sb("att_cols", [P, 4], F32)
        score_w = sb("score_w", [P, 4, P], F32)
        conv_w = sb("conv_w", [P, 4, C], F32)
        conv_b = sb("conv_b", [P, 2], F32)

        xs = [sb(f"xs{q}", [P, T, C], F32) for q in range(2)]
        kinds = [sb(f"kinds{q}", [P, T, N], BF16) for q in range(2)]
        h0 = [sb(f"h0_{q}", [P, T, C], F32) for q in range(2)]
        agg = sb("agg", [P, T, C], F32)

        raw = sb("raw", [P, 2, N], I32)
        key = sb("key", [P, 2, N], F16)
        top = sb("top", [P, T, 8 * ROUNDS], F16)
        ones_h = sb("ones_h", [P, 1], F16)
        occupied = sb("occupied", [1, T, PAIRS], F32)
        pairs_sum = sb("pairs_sum", [1, T], F32)
        wanted = sb("wanted", [1, T], I32)
        idx = sb("idx", [P, T, 8 * ROUNDS], U32)
        gath = sb("gath", [P, GSLOTS, SAMPLES * C], F32)

        mask = sb("mask", [P, T, N], BF16)
        maskT = sb("maskT", [P, T, N], BF16)
        hn = sb("hn", [P, T, C], F32)
        hT = sb("hT", [P, N], F32)
        aggT = sb("aggT", [P, N], F32)
        gn = sb("gn", [P, T, C], F32)
        rowneg = sb("rowneg", [P, N], F32)
        rowneg02 = sb("rowneg02", [P, N], F32)
        colneg = sb("colneg", [P, T], F32)
        degree = sb("degree", [P, T], F32)
        rdegree = sb("rdegree", [P, T], F32)
        tmp = sb("tmp", [P, N], F32)
        att_wide = tmp[:, 0:4 * P].rearrange("p (a c) -> p a c", a=4)
        score = sb("score", [P, 2, N], F32)
        prob = sb("prob", [P, 2, N], F32)
        probT = sb("probT", [P, 2, N], F32)
        negmax = sb("negmax", [P, T], F32)
        total = sb("total", [P, T], F32)
        rtotal = sb("rtotal", [P, T], F32)
        gz = sb("gz", [P, 2, C], F32)
        parts = score[:, :, :].bitcast(BF16).rearrange("p a n -> p (a n)")[:, 0:3 * N].rearrange("p (a n) -> p a n", a=3)
        ideg = probT[:, 0, :]
        pos = probT[:, 1, :]
        rest = prob[:, 0, :]
        ebuf = prob[:, 1, :]
        hcT = sb("hcT", [P, N], F32)
        stats = sb("stats", [P, 2, T, 6], F32)
        mv = sb("mv", [P, 2, T, 2], F32)
        var = sb("var", [P, 2, T], F32)
        root = sb("root", [P, 2, T], F32)
        shift = sb("shift", [P, 2, T], F32)
        conv_negb = sb("conv_negb", [P, 2], F32)
        half = sb("half", [P, 2, T], F32)
        sq = sb("sq", [P, 2, T], F32)

        psA, psB, psC, psD = [ctx.enter_context(nc.psum_tensor(n, [P, N], F32)) for n in ("psA", "psB", "psC", "psD")]
        psDb = psD[:, :].bitcast(BF16).rearrange("p (h t i) -> p h t i", h=2, t=T)

        consts_ready = sem("consts_ready")
        weights_in = sem("weights_in")
        wT_ps = sem("wT_ps")
        wT_sb = sem("wT_sb")
        att_wide_ready = sem("att_wide_ready")
        score_w_ps = sem("score_w_ps")
        score_w_sb = sem("score_w_sb")
        zero_stored = sem("zero_stored")
        sp_turn = sem("sp_turn")
        dve_turn = sem("dve_turn")
        pool_turn = sem("pool_turn")
        x_in = sem("x_in")
        adj_in = [sem(f"adj_in{i}") for i in range(2)]
        raw_used = sem("raw_used")
        kinds_sb = sem("kinds_sb")
        x0_in = sem("x0_in")
        norm0_ready = sem("norm0_ready")
        norm_ready = sem("norm_ready")
        h0_ready = sem("h0_ready")
        h0_stored = sem("h0_stored")
        idx_ready = sem("idx_ready")
        occupied_ps = sem("occupied_ps")
        wanted_ready = sem("wanted_ready")
        gathered = [sem(f"gathered{i}") for i in range(GSLOTS)]
        reduced = sem("reduced")
        h0T_ps = sem("h0T_ps")
        aggT_ps = sem("aggT_ps")
        hT_sb = sem("hT_sb")
        aggT_sb = sem("aggT_sb")
        lin0_ps = sem("lin0_ps")
        mask_ready = sem("mask_ready")
        maskT_ps = sem("maskT_ps")
        maskT_sb = sem("maskT_sb")
        hn_ready = sem("hn_ready")
        hnT_ps = sem("hnT_ps")
        rows_ps = sem("rows_ps")
        columns_ps = sem("columns_ps")
        scores_sb = sem("scores_sb")
        proj_ps = sem("proj_ps")
        proj_sb = sem("proj_sb")
        score_ready = sem("score_ready")
        prob_sb = sem("prob_sb")
        rtotal_ready = sem("rtotal_ready")
        gz_ready = sem("gz_ready")
        pv_done = sem("pv_done")
        att1_ps = sem("att1_ps")
        elu_arg = sem("elu_arg")
        elu_sb = sem("elu_sb")
        probT_ps = sem("probT_ps")
        probT_sb = sem("probT_sb")
        ctx_done = sem("ctx_done")
        part_sb = sem("part_sb")
        rest_ready = sem("rest_ready")
        degree_ps = sem("degree_ps")
        rdegree_ready = sem("rdegree_ready")
        ideg_ps = sem("ideg_ps")
        ideg_sb = sem("ideg_sb")
        neigh_ps = sem("neigh_ps")
        neighT_sb = sem("neighT_sb")
        conv_ps = sem("conv_ps")
        hc_ready = sem("hc_ready")
        hc_ps = sem("hc_ps")
        x_final = sem("x_final")
        out_stored = sem("out_stored")
        dve_step = sem("dve_step")

        x_v = x.rearrange("b (t p) c -> b p t c", p=P)
        out_v = out.rearrange("b (t p) c -> b p t c", p=P)
        adj_v = adj.rearrange("b (t p) j -> b t p j", p=P)
        SPARSE = ((4,), (5, 6), (7,))

        def pair_counts(t):
            return psD[0:1, HALF + PAIRS * (t - 4):HALF + PAIRS * (t - 3)]

        COLS = [slice(h * HALF, (h + 1) * HALF) for h in range(N // HALF)]
        TILES = [range(h * T // 2, (h + 1) * T // 2) for h in range(2)]

        block = ctx.enter_context(nc.Block())


        @block.sync
        def _(sp):
            def load_x0(g, q):
                sp.dma_start(h0[q][:, :, :], x_v[g]).then_inc(x0_in, 16)

            def load_x(g, q):
                sp.dma_start(xs[q][:, :, :], x_v[g]).then_inc(x_in, 16)

            def store_h0(g, q):
                sp.wait_ge(h0_ready, g + 1)
                sp.sem_inc(sp_turn, 1)
                sp.dma_start(h0_rows[q][0:N].rearrange("(t p) c -> p t c", p=P), h0[q][:, :, :]).then_inc(h0_stored, 16)

            def load_adj(g, t, first=False):
                if not first:
                    sp.wait_ge(raw_used, 8 * g + t - 1)
                    sp.sem_inc(sp_turn, 1)
                    sp.wait_ge(kinds_sb, 8 * g + t - 1)
                    sp.sem_inc(sp_turn, 1)
                sp.dma_start(raw[:, t % 2, :], adj_v[g, t]).then_inc(adj_in[t % 2], 16)

            load_x0(0, 0)
            load_adj(0, 0, first=True)
            load_adj(0, 1, first=True)
            sp.wait_ge(consts_ready, 1)
            for q in range(2):
                sp.dma_start(h0_rows[q][N:N + 1, :], zero_row[0:1, :]).then_inc(zero_stored, 16)
            store_h0(0, 0)
            sp.wait_ge(consts_ready, 3)
            sp.dma_start(blank[:, :], gath[:, GSLOTS - 1, 0:2 * PAIRS * C]).then_inc(zero_stored, 16)
            load_adj(0, 2)
            for dst, src in (
                (w0[:, 0, :], L0_gnn_W[0:C]), (w0[:, 1, :], L0_gnn_W[C:2 * C]),
                (w1[:, :], L1_gnn_W), (w2[:, :], L2_gnn_W),
                (att_cols[:, 0:1], L1_gnn_a[0:C]), (att_cols[:, 1:2], L1_gnn_a[C:2 * C]),
                (att_cols[:, 2:3], L2_gnn_a[:, C:2 * C].rearrange("a o -> o a")),
                (att_cols[:, 3:4], L2_gnn_a[:, 0:C].rearrange("a o -> o a")),
                (conv_w[:, 0, :], L3_gnn_w_root1), (conv_w[:, 1, :], L3_gnn_w_rel1[1]),
                (conv_w[:, 2, :], L3_gnn_w_root2), (conv_w[:, 3, :], L3_gnn_w_rel2[1]),
                (conv_b[:, 0:1], L3_gnn_b1.rearrange("(o a) -> o a", a=1)),
                (conv_b[:, 1:2], L3_gnn_b2.rearrange("(o a) -> o a", a=1)),
            ):
                sp.dma_start(dst, src).then_inc(weights_in, 16)
            for r in range(HALF // C):
                sp.dma_start(b0_row[0:1, r * C:(r + 1) * C], L0_gnn_b.rearrange("(a o) -> a o", a=1)).then_inc(weights_in, 16)
            load_x(0, 0)
            for t in range(3, T):
                load_adj(0, t)
            load_x0(1, 1)
            load_adj(1, 0)
            store_h0(1, 1)
            load_adj(1, 1)
            load_adj(1, 2)
            load_adj(1, 3)
            load_adj(1, 4)
            load_x(1, 1)

            def iteration(g, q, ahead=2):
                if ahead >= 2:
                    sp.wait_ge(h0T_ps, g + 1)
                    sp.sem_inc(sp_turn, 1)
                    load_x0(g + 2, q)
                if ahead >= 1:
                    for t in range(5, T):
                        load_adj(g + 1, t)
                if ahead >= 2:
                    load_adj(g + 2, 0)
                    sp.wait_ge(reduced, 8 * g + 8)
                    sp.sem_inc(sp_turn, 1)
                    store_h0(g + 2, q)
                    load_adj(g + 2, 1)
                    load_adj(g + 2, 2)
                    load_adj(g + 2, 3)
                    load_adj(g + 2, 4)
                sp.wait_ge(x_final, g + 2)
                sp.sem_inc(sp_turn, 1)
                sp.dma_start(out_v[g], xs[q][:, :, :]).then_inc(out_stored, 16)
                if ahead >= 2:
                    sp.wait_ge(out_stored, 16 * g + 16)
                    sp.sem_inc(sp_turn, 1)
                    load_x(g + 2, q)

            with sp.Fori(0, (B - 2) // 2) as pair:
                for q in range(2):
                    iteration(pair * 2 + q, q)
            iteration(B - 2, 0, ahead=1)
            iteration(B - 1, 1, ahead=0)
            sp.wait_ge(out_stored, 16 * B)

        @block.gpsimd
        def _(pool):
            nc.gpsimd.memset(zero_row[:, :], 0.0)
            nc.gpsimd.memset(ones_h[:, :], 1.0)
            nc.gpsimd.memset(ones[:, :], 1.0)
            nc.gpsimd.memset(ones_bf[:, :], 1.0)
            nc.gpsimd.iota(countdown[:, :], pattern=[[-1, N]], base=N, channel_multiplier=0,
                           allow_small_or_imprecise_dtypes=True)
            nc.gpsimd.memset(ident[:, :], 0.0).then_inc(consts_ready, 1)
            pool.wait_ge(consts_ready, 1)
            nc.gpsimd.affine_select(out=ident[:, :], in_=ident[:, :], compare_op=ALU.not_equal, fill=1.0, base=0,
                                    pattern=[[-1, P]], channel_multiplier=1).then_inc(consts_ready, 1)
            pool.wait_ge(consts_ready, 2)
            nc.gpsimd.memset(gath[:, GSLOTS - 1, 0:2 * PAIRS * C], 0.0)
            nc.gpsimd.tensor_copy(ident_bf[:, :], ident[:, :]).then_inc(consts_ready, 1)
            pool.wait_ge(zero_stored, 48)

            def gather_slot(q, t, s):
                nc.gpsimd.indirect_dma_start(
                    out=gath[:, t % GSLOTS, s * C:(s + 1) * C], out_offset=None, in_=h0_rows[q][:, :],
                    in_offset=bass.IndirectOffsetOnAxis(ap=idx[:, t, s:s + 1], axis=0),
                ).then_inc(gathered[t % GSLOTS], 16)

            def gather(g, q, first=False):
                pool.wait_ge(h0_stored, 16 * g + 16)
                for t in range(T):
                    pool.wait_ge(idx_ready, 8 * g + t + 1)
                    if not (first and t < GSLOTS):
                        pool.wait_ge(reduced, 8 * g + (-1, 0, -2, 1, 2, 3, 4, 5)[t])
                    pool.sem_inc(pool_turn, 1)
                    done = gathered[t % GSLOTS]
                    for s in range(ALWAYS if t >= 4 else SAMPLES):
                        gather_slot(q, t, s)
                    if t < 4:
                        continue
                    pool.wait_ge(wanted_ready, 3 * g + (1, 2, 2, 3)[t - 4])
                    pool.sem_inc(pool_turn, 1)
                    pairs = pool.value_load(wanted[0:1, t:t + 1], min_val=0, max_val=PAIRS)
                    for k in range(PAIRS):
                        with pool.If(pairs > k):
                            gather_slot(q, t, ALWAYS + 2 * k)
                            gather_slot(q, t, ALWAYS + 2 * k + 1)
                    for k in range(PAIRS):
                        with pool.If(pairs == k):
                            nc.gpsimd.dma_start(gath[:, t % GSLOTS, (ALWAYS + 2 * k) * C:SAMPLES * C],
                                                blank[:, 0:2 * (PAIRS - k) * C]).then_inc(done, 32 * (PAIRS - k))

            gather(0, 0, first=True)
            with pool.Fori(0, (B - 2) // 2) as pair:
                gather(pair * 2 + 1, 1)
                gather(pair * 2 + 2, 0)
            gather(B - 1, 1)

        @block.scalar
        def _(act):
            def projections(g, layer):
                for h in range(2):
                    act.wait_ge(hnT_ps, 6 * g + 2 * layer + h + 1)
                    nc.scalar.activation(hT[:, COLS[h]], psB[:, COLS[h]], ACT.Relu).then_inc(hT_sb, 1)
                act.wait_ge(rows_ps, 2 * g + 1 + layer)
                nc.scalar.mul(rowneg[:, :], psC[:, :], -1.0)
                nc.scalar.mul(rowneg02[:, :], psC[:, :], -SLOPE)
                act.wait_ge(columns_ps, 2 * g + 1 + layer)
                nc.scalar.mul(colneg[:, :], psD[:, 0:T], SLOPE - 1.0).then_inc(scores_sb, 1)
                act.wait_ge(proj_ps, 2 * g + 1 + layer)
                nc.scalar.copy(gn[:, :, :].rearrange("p t c -> p (t c)"), psA[:, :]).then_inc(proj_sb, 1)

            def softmax(g, layer, t):
                n = 8 * layer + t
                act.wait_ge(score_ready, 16 * g + n + 1)
                if layer == 0 and t >= 2:
                    act.wait_ge(pv_done, 8 * g + t - 1)
                if layer == 1 and t >= 2:
                    act.wait_ge(probT_ps, 8 * g + t - 1)
                nc.scalar.activation(prob[:, t % 2, :], score[:, t % 2, :], ACT.Exp, bias=negmax[:, t:t + 1],
                                     scale=-1.0, accum_out=total[:, t:t + 1]).then_inc(prob_sb, 1)

            def scale_rows(g, t):
                if t == 0:
                    act.wait_ge(proj_sb, 2 * g + 1)
                if t >= 2:
                    act.wait_ge(pv_done, 8 * g + t - 1)
                act.wait_ge(rtotal_ready, 8 * g + t + 1)
                nc.scalar.activation(gz[:, t % 2, :], gn[:, t, :], ACT.Copy, scale=rtotal[:, t:t + 1]).then_inc(gz_ready, 1)

            def move_maskT(g):
                for t in range(T):
                    act.wait_ge(maskT_ps, 8 * g + t + 1)
                    nc.scalar.copy(maskT[:, :, t * P:(t + 1) * P], psDb[:, t % 2]).then_inc(maskT_sb, 1)

            def move_probT(g, t):
                act.wait_ge(probT_ps, 8 * g + t + 1)
                if t >= 2:
                    act.wait_ge(ctx_done, 8 * g + t - 1)
                nc.scalar.copy(probT[:, t % 2, :], (psB, psC)[t % 2][:, :]).then_inc(probT_sb, 1)

            def copy_kinds(g, q, t):
                act.wait_ge(adj_in[t % 2], 16 * (4 * g + t // 2 + 1))
                nc.scalar.copy(kinds[q][:, t, :], raw[:, t % 2, :]).then_inc(kinds_sb, 1)

            def normalise0(g, q):
                for t in range(T):
                    last = nc.scalar.activation(h0[q][:, t, :], h0[q][:, t, :], ACT.Relu, bias=shift[:, 1, t:t + 1],
                                                scale=root[:, 1, t:t + 1])
                last.then_inc(h0_ready, 1)

            def normalise_x(g, q, layer):
                act.wait_ge(norm_ready, 3 * g + layer)
                for h in range(2):
                    for t in TILES[h]:
                        last = nc.scalar.activation(hn[:, t, :], xs[q][:, t, :], ACT.Identity, bias=shift[:, 0, t:t + 1],
                                                    scale=root[:, 0, t:t + 1])
                    last.then_inc(hn_ready, 1)

            def elu(g, n):
                src = psC if n == 0 else psD
                for h in range(2):
                    if n == 0:
                        act.wait_ge(att1_ps, 2 * g + h + 1)
                    else:
                        act.wait_ge(conv_ps, 4 * g + 2 * (n - 1) + h + 1)
                    nc.scalar.activation(ebuf[:, COLS[h]], src[:, COLS[h]], ACT.Relu, scale=-1.0,
                                         bias=0.0 if n == 0 else conv_negb[:, n - 1:n]).then_inc(elu_arg, 1)
                    if n > 0:
                        nc.scalar.activation(pos[:, COLS[h]], src[:, COLS[h]], ACT.Relu, bias=conv_b[:, n - 1:n])
                    act.wait_ge(elu_arg, 6 * g + 2 * n + h + 1)
                    nc.scalar.activation(ebuf[:, COLS[h]], ebuf[:, COLS[h]], ACT.Exp, scale=-1.0).then_inc(elu_sb, 1)

            def split(g, n):
                for h in range(2):
                    if n == 0:
                        act.wait_ge(hn_ready, 6 * g + 4 + h + 1)
                        nc.scalar.activation(parts[:, 0, COLS[h]], hn[:, :, :].rearrange("p t c -> p (t c)")[:, COLS[h]],
                                             ACT.Relu).then_inc(part_sb, 1)
                    else:
                        act.wait_ge(hc_ps, 4 * g + h + 1)
                        nc.scalar.copy(parts[:, 0, COLS[h]], psB[:, COLS[h]]).then_inc(part_sb, 1)
                for k in range(1, 3):
                    for h in range(2):
                        act.wait_ge(rest_ready, 8 * g + 4 * n + 2 * (k - 1) + h + 1)
                        nc.scalar.copy(parts[:, k, COLS[h]], (rest, tmp)[k - 1][:, COLS[h]]).then_inc(part_sb, 1)

            def iteration(g, q, ahead=2):
                o = 1 - q
                act.wait_ge(h0T_ps, g + 1)
                nc.scalar.copy(hT[:, :], psB[:, :]).then_inc(hT_sb, 1)
                if ahead >= 1:
                    copy_kinds(g + 1, o, 3)
                if ahead >= 1:
                    move_maskT(g)
                for h in range(2):
                    act.wait_ge(aggT_ps, 2 * g + h + 1)
                    nc.scalar.copy(aggT[:, COLS[h]], psC[:, COLS[h]]).then_inc(aggT_sb, 1)
                if ahead == 0:
                    move_maskT(g)
                if ahead >= 1:
                    normalise_x(g, q, 1)
                    copy_kinds(g + 1, o, 4)
                projections(g, 0)
                if ahead >= 1:
                    copy_kinds(g + 1, o, 5)
                for t in range(T):
                    softmax(g, 0, t)
                    if t >= 1:
                        scale_rows(g, t - 1)
                scale_rows(g, T - 1)
                act.wait_ge(pv_done, 8 * g + T)
                for h in range(2):
                    nc.scalar.copy(hT[:, COLS[h]], psB[:, COLS[h]]).then_inc(hT_sb, 1)
                elu(g, 0)
                if ahead >= 1:
                    normalise_x(g, q, 2)
                    copy_kinds(g + 1, o, 6)
                projections(g, 1)
                if ahead >= 1:
                    copy_kinds(g + 1, o, 7)
                for t in range(T):
                    softmax(g, 1, t)
                    if t >= 1:
                        move_probT(g, t - 1)
                move_probT(g, T - 1)
                if ahead >= 1:
                    normalise_x(g, q, 3)
                for h in range(2):
                    act.wait_ge(hnT_ps, 6 * g + 4 + h + 1)
                    nc.scalar.activation(hT[:, COLS[h]], psB[:, COLS[h]], ACT.Relu).then_inc(hT_sb, 1)
                split(g, 0)
                act.wait_ge(ideg_ps, g + 1)
                nc.scalar.copy(ideg, psC[:, :]).then_inc(ideg_sb, 1)
                if ahead >= 2:
                    normalise0(g + 2, q)
                    act.wait_ge(mask_ready, 3 * g + 3)
                    copy_kinds(g + 2, q, 0)
                elu(g, 1)
                split(g, 1)
                if ahead >= 2:
                    copy_kinds(g + 2, q, 1)
                    copy_kinds(g + 2, q, 2)
                elu(g, 2)

            copy_kinds(0, 0, 0)
            act.wait_ge(norm0_ready, 1)
            normalise0(0, 0)
            for t in range(1, T):
                copy_kinds(0, 0, t)
            act.wait_ge(wT_ps, 1)
            nc.scalar.copy(w1T[:, :], psA[:, 0:P])
            nc.scalar.copy(w2T[:, :], psA[:, P:2 * P]).then_inc(wT_sb, 1)
            act.wait_ge(score_w_ps, 1)
            nc.scalar.copy(score_w[:, :, :].rearrange("p a c -> p (a c)"), psB[:, 0:HALF]).then_inc(score_w_sb, 1)
            nc.scalar.mul(conv_negb[:, :], conv_b[:, :], -1.0)
            act.wait_ge(norm0_ready, 2)
            normalise0(1, 1)
            for t in range(3):
                copy_kinds(1, 1, t)
            with act.Fori(0, (B - 2) // 2) as pair:
                for q in range(2):
                    iteration(pair * 2 + q, q)
            iteration(B - 2, 0, ahead=1)
            iteration(B - 1, 1, ahead=0)

        @block.vector
        def _(dve):
            chain = {"n": 0}

            def step(ins):
                chain["n"] += 1
                ins.then_inc(dve_step, 1)
                return chain["n"]

            def link(ins):
                dve.wait_ge(dve_step, step(ins))

            def restart_links():
                dve.sem_clear(dve_step)
                chain["n"] = 0

            V = nc.vector

            def flat(a):
                return a.rearrange("p t c -> p (t c)")

            def moments(*sources):
                w = slice(sources[0][0], sources[-1][0] + 1)
                y, m, v, hv, sv = root[:, w, :], shift[:, w, :], var[:, w, :], half[:, w, :], sq[:, w, :]
                for which, src in sources:
                    for t in range(T):
                        last = V.bn_stats(stats[:, which, t, :], src[:, t, :])
                link(last)
                for which, src in sources:
                    for t in range(T):
                        last = V.bn_aggr(mv[:, which, t, :], stats[:, which, t, :])
                link(last)
                link(V.tensor_scalar(v, mv[:, w, :, 1], EPS, None, ALU.add))
                V.tensor_scalar(y.bitcast(I32), v.bitcast(I32), -0.5, ROOT_SEED, ALU.mult, ALU.add)
                link(V.tensor_scalar(hv, v, -0.5, None, ALU.mult))
                for _ in range(3):
                    link(V.tensor_tensor(sv, y, y, ALU.mult))
                    link(V.tensor_tensor(sv, sv, hv, ALU.mult))
                    link(V.scalar_tensor_tensor(out=y, in0=sv, scalar=1.5, in1=y, op0=ALU.add, op1=ALU.mult))
                return V.scalar_tensor_tensor(out=m, in0=mv[:, w, :, 0], scalar=-1.0, in1=y, op0=ALU.mult, op1=ALU.mult)

            last_pass = {}
            PASSES = 2 * ROUNDS + 1

            def select_pass(g, t, n):
                keys = key[:, t % 2, :]
                if n == 0:
                    dve.wait_ge(adj_in[t % 2], 16 * (4 * g + t // 2 + 1))
                    last = V.scalar_tensor_tensor(out=keys, in0=raw[:, t % 2, :], scalar=0.0, in1=countdown[:, :],
                                                  op0=ALU.not_equal, op1=ALU.mult)
                    last_pass[t] = step(last)
                    return
                dve.wait_ge(dve_step, last_pass[t])
                eight = slice(8 * ((n - 1) // 2), 8 * ((n - 1) // 2) + 8)
                if n == PASSES - 1:
                    V.tensor_scalar(idx[:, t, :], top[:, t, :], -1.0, float(N), ALU.mult, ALU.add).then_inc(idx_ready, 1)
                elif n % 2 == 1:
                    if n == 1:
                        dve.sem_inc(raw_used, 1)
                    last_pass[t] = step(V.max(top[:, t, eight], keys))
                else:
                    last_pass[t] = step(V.match_replace(keys, top[:, t, eight], keys, 0.0))

            def select(g, tiles, passes=range(PASSES)):
                for n in passes:
                    for t in tiles:
                        select_pass(g, t, n)

            def count_pairs(g, batch):
                tiles = SPARSE[batch]
                rows = slice(tiles[0], tiles[-1] + 1)
                dve.wait_ge(occupied_ps, 3 * g + batch + 1)
                for t in tiles:
                    last = V.tensor_scalar(occupied[:, t, :], pair_counts(t), 0.0, None, ALU.is_gt)
                link(last)
                link(V.tensor_reduce(out=pairs_sum[:, rows], in_=occupied[:, rows, :], axis=AX_X, op=ALU.add))
                V.tensor_copy(wanted[:, rows], pairs_sum[:, rows]).then_inc(wanted_ready, 1)

            def reduce(g, t):
                slot = t % GSLOTS
                dve.wait_ge(gathered[slot], 16 * SAMPLES * ((3, 3, 2)[slot] * g + t // GSLOTS + 1))
                V.tensor_reduce(out=agg[:, t, :], in_=gath[:, slot, :].rearrange("p (s c) -> p c s", c=C),
                                axis=AX_X, op=ALU.max).then_inc(reduced, 1)

            def head(g, q):
                dve.wait_ge(x0_in, 16 * g + 16)
                moments((1, h0[q])).then_inc(norm0_ready, 1)

            def leaky(g, layer, t):
                if t >= 2:
                    dve.wait_ge(score_ready, 16 * g + 8 * layer + t - 1)
                return step(V.scalar_tensor_tensor(out=(tmp, hcT)[t % 2][:, :], in0=rowneg[:, :], scalar=colneg[:, t:t + 1],
                                                   in1=rowneg02[:, :], op0=ALU.add, op1=ALU.min))

            def masked(g, layer, t, made):
                n = 8 * layer + t
                if n >= 2:
                    dve.wait_ge(prob_sb, 16 * g + n - 1)
                    dve.sem_inc(dve_turn, 1)
                dve.wait_ge(dve_step, made)
                V.tensor_tensor_reduce(out=score[:, t % 2, :], in0=(tmp, hcT)[t % 2][:, :], in1=(maskT, mask)[layer][:, t, :],
                                       scale=1.0, scalar=3e38, op0=ALU.add, op1=ALU.min,
                                       accum_out=negmax[:, t:t + 1]).then_inc(score_ready, 1)

            def attention(g, layer, ahead, t_ahead):
                if ahead:
                    select_pass(g + 1, t_ahead, 0)
                made = leaky(g, layer, 0)
                for t in range(T):
                    after = leaky(g, layer, t + 1) if t + 1 < T else None
                    masked(g, layer, t, made)
                    made = after
                    if ahead:
                        select_pass(g + 1, t_ahead, t + 1)
                        if t == 3:
                            count_pairs(g + 1, layer)
                    if layer == 0 and 1 <= t < T - 1:
                        invert_sum(g, t - 1)

            def invert_sum(g, t):
                dve.wait_ge(prob_sb, 16 * g + t + 1)
                V.reciprocal(rtotal[:, t:t + 1], total[:, t:t + 1]).then_inc(rtotal_ready, 1)

            def split(g, n):
                for h in range(2):
                    dve.wait_ge(part_sb, 12 * g + 6 * n + h + 1)
                    if n == 0:
                        last = V.scalar_tensor_tensor(out=rest[:, COLS[h]], in0=flat(hn[:, :, :])[:, COLS[h]], scalar=0.0,
                                                      in1=parts[:, 0, COLS[h]], op0=ALU.max, op1=ALU.subtract)
                    else:
                        last = V.tensor_tensor(rest[:, COLS[h]], psB[:, COLS[h]], parts[:, 0, COLS[h]], ALU.subtract)
                    last.then_inc(rest_ready, 1)
                for h in range(2):
                    dve.wait_ge(part_sb, 12 * g + 6 * n + 2 + h + 1)
                    V.tensor_tensor(tmp[:, COLS[h]], rest[:, COLS[h]], parts[:, 1, COLS[h]], ALU.subtract).then_inc(rest_ready, 1)

            def divide(g, n):
                if n == 0:
                    dve.wait_ge(ideg_sb, g + 1)
                for h in range(2):
                    dve.wait_ge(neigh_ps, 4 * g + 2 * n + h + 1)
                    V.tensor_tensor(aggT[:, COLS[h]], psA[:, COLS[h]], ideg[:, COLS[h]], ALU.mult).then_inc(neighT_sb, 1)

            def elu(g, n):
                for h in range(2):
                    dve.wait_ge(elu_sb, 6 * g + 2 * n + h + 3)
                    V.scalar_tensor_tensor(out=hcT[:, COLS[h]], in0=ebuf[:, COLS[h]], scalar=-1.0, in1=pos[:, COLS[h]],
                                           op0=ALU.add, op1=ALU.add).then_inc(hc_ready, 1)

            def norm(q, ahead, coming=False):
                last = moments((0, xs[q]), (1, h0[q])) if coming else moments((0, xs[q]))
                if ahead >= 1:
                    last.then_inc(norm_ready, 1)
                    return
                link(last)
                for h in range(2):
                    for t in TILES[h]:
                        last = V.tensor_scalar(hn[:, t, :], xs[q][:, t, :], root[:, 0, t:t + 1], shift[:, 0, t:t + 1],
                                               ALU.mult, ALU.add)
                    last.then_inc(hn_ready, 1)

            def iteration(g, q, ahead=2):
                X = flat(xs[q][:, :, :])
                restart_links()
                V.tensor_scalar(flat(mask[:, :, :]), flat(kinds[q][:, :, :]), 0.0, BIG, ALU.is_le, ALU.mult).then_inc(mask_ready, 1)
                if ahead == 0:
                    reduce(g, 7)
                if ahead >= 1:
                    select(g + 1, (3, 4), range(0, 5))
                dve.wait_ge(x_in, 16 * g + 16)
                for h in range(2):
                    dve.wait_ge(lin0_ps, 2 * g + h + 1)
                    last = V.scalar_tensor_tensor(out=X[:, COLS[h]], in0=psA[:, COLS[h]], scalar=0.0, in1=X[:, COLS[h]],
                                                  op0=ALU.max, op1=ALU.add)
                link(last)
                norm(q, ahead)
                if ahead >= 1:
                    reduce(g + 1, 0)
                    select(g + 1, (3, 4), range(5, PASSES))
                dve.wait_ge(maskT_sb, 8 * g + T)
                dve.wait_ge(scores_sb, 2 * g + 1)
                attention(g, 0, ahead >= 1, 5)
                V.tensor_scalar(flat(mask[:, :, :]), flat(kinds[q][:, :, :]), 0.0, BIG, ALU.is_equal, ALU.mult).then_inc(mask_ready, 1)
                invert_sum(g, T - 2)
                invert_sum(g, T - 1)
                if ahead >= 1:
                    reduce(g + 1, 1)
                    reduce(g + 1, 2)
                above = []
                for h in range(2):
                    dve.wait_ge(elu_arg, 6 * g + h + 1)
                    above.append(step(V.scalar_tensor_tensor(out=X[:, COLS[h]], in0=psC[:, COLS[h]], scalar=0.0,
                                                             in1=X[:, COLS[h]], op0=ALU.max, op1=ALU.add)))
                for h in range(2):
                    dve.wait_ge(dve_step, above[h])
                    dve.wait_ge(elu_sb, 6 * g + h + 1)
                    last = V.scalar_tensor_tensor(out=X[:, COLS[h]], in0=ebuf[:, COLS[h]], scalar=-1.0, in1=X[:, COLS[h]],
                                                  op0=ALU.add, op1=ALU.add)
                link(last)
                norm(q, ahead)
                if ahead >= 1:
                    select(g + 1, (6,))
                    reduce(g + 1, 3)
                dve.wait_ge(mask_ready, 3 * g + 2)
                dve.wait_ge(scores_sb, 2 * g + 2)
                attention(g, 1, ahead >= 1, 7)
                dve.wait_ge(score_ready, 16 * g + 16)
                V.tensor_scalar(flat(mask[:, :, :]), flat(kinds[q][:, :, :]), 1.0, None, ALU.is_equal).then_inc(mask_ready, 1)
                if ahead >= 1:
                    reduce(g + 1, 4)
                dve.wait_ge(prob_sb, 16 * g + 16)
                link(V.reciprocal(rtotal[:, :], total[:, :]))
                dve.wait_ge(ctx_done, 8 * g + T)
                for t in range(T):
                    last = V.scalar_tensor_tensor(out=xs[q][:, t, :], in0=psA[:, t * P:(t + 1) * P],
                                                  scalar=rtotal[:, t:t + 1], in1=xs[q][:, t, :], op0=ALU.mult, op1=ALU.add)
                link(last)
                if ahead >= 2:
                    dve.wait_ge(x0_in, 16 * g + 48)
                norm(q, ahead, coming=ahead >= 2)
                if ahead >= 1:
                    count_pairs(g + 1, 2)
                dve.wait_ge(degree_ps, g + 1)
                link(V.tensor_scalar(degree[:, :], psD[:, T:2 * T], 1.0, None, ALU.max))
                V.reciprocal(rdegree[:, :], degree[:, :]).then_inc(rdegree_ready, 1)
                if ahead >= 2:
                    select(g + 2, (0,), range(0, 4))
                split(g, 0)
                if ahead >= 2:
                    select(g + 2, (0,), range(4, PASSES))
                if ahead >= 1:
                    reduce(g + 1, 5)
                divide(g, 0)
                if ahead >= 1:
                    reduce(g + 1, 6)
                elu(g, 0)
                if ahead >= 2:
                    select(g + 2, (1, 2), range(0, 3))
                split(g, 1)
                if ahead >= 2:
                    select(g + 2, (1, 2), range(3, PASSES))
                divide(g, 1)
                if ahead >= 2:
                    reduce(g + 1, 7)
                elu(g, 1)
                for h in range(2):
                    dve.wait_ge(hc_ps, 4 * g + 2 + h + 1)
                    last = V.tensor_tensor(X[:, COLS[h]], psB[:, COLS[h]], X[:, COLS[h]], ALU.add)
                last.then_inc(x_final, 1)

            dve.sem_inc(x_final, 1)
            dve.wait_ge(consts_ready, 3)
            head(0, 0)
            select(0, (0,))
            select(0, (1,))
            dve.wait_ge(weights_in, 16 * 18)
            for a in range(4):
                last = V.tensor_scalar(att_wide[:, a, :], ones[:, :], att_cols[:, a:a + 1], None, ALU.mult)
            last.then_inc(att_wide_ready, 1)
            for t in range(2, T):
                select(0, (t,))
                if t == 6:
                    count_pairs(0, 0)
                if t >= 3:
                    reduce(0, t - 3)
            count_pairs(0, 1)
            count_pairs(0, 2)
            head(1, 1)
            select(1, (0,))
            reduce(0, 5)
            select(1, (1,))
            reduce(0, 6)
            select(1, (2,))
            reduce(0, 7)
            with dve.Fori(0, (B - 2) // 2) as pair:
                for q in range(2):
                    iteration(pair * 2 + q, q)
            iteration(B - 2, 0, ahead=1)
            iteration(B - 1, 1, ahead=0)

        @block.tensor
        def _(pe):
            def transposes(dst, src, identity):
                for t in range(T):
                    last = nc.tensor.transpose(dst[:, t * P:(t + 1) * P], src[:, t * P:(t + 1) * P], identity)
                return last

            def flat(a):
                return a.rearrange("p t c -> p (t c)")

            pe.wait_ge(weights_in, 16 * 18)
            pe.wait_ge(consts_ready, 3)
            nc.tensor.transpose(psA[:, 0:P], w1[:, :], ident[:, :])
            nc.tensor.transpose(psA[:, P:2 * P], w2[:, :], ident[:, :]).then_inc(wT_ps, 1)
            pe.wait_ge(wT_sb, 1)
            pe.wait_ge(att_wide_ready, 1)
            nc.tensor.matmul(psB[:, 0:2 * P], w1T[:, :], flat(att_wide[:, 0:2, :]), start=True, stop=True)
            nc.tensor.matmul(psB[:, 2 * P:4 * P], w2[:, :], flat(att_wide[:, 2:4, :]), start=True, stop=True).then_inc(score_w_ps, 1)
            pe.wait_ge(score_w_sb, 1)

            def transpose_half(dst, src, h):
                for t in TILES[h]:
                    last = nc.tensor.transpose(dst[:, t * P:(t + 1) * P], src[:, t * P:(t + 1) * P], ident[:, :])
                return last

            def project(g, layer):
                weight = (w1, w2T)[layer]
                for h in range(2):
                    pe.wait_ge(hn_ready, 6 * g + 2 * layer + h + 1)
                    transpose_half(psB, flat(hn[:, :, :]), h).then_inc(hnT_ps, 1)
                for h in range(2):
                    pe.wait_ge(hT_sb, 9 * g + 4 * layer + h + 2)
                    last = nc.tensor.matmul(psC[:, COLS[h]], score_w[:, 2 * layer, :], hT[:, COLS[h]], start=True, stop=True)
                last.then_inc(rows_ps, 1)
                for t in range(T):
                    last = nc.tensor.matmul(psD[:, t:t + 1], hT[:, t * P:(t + 1) * P], score_w[:, 2 * layer + 1, 0:1], start=True, stop=True)
                last.then_inc(columns_ps, 1)
                for t in range(T):
                    last = nc.tensor.matmul(psA[:, t * P:(t + 1) * P], hT[:, t * P:(t + 1) * P], weight[:, :], start=True, stop=True)
                last.then_inc(proj_ps, 1)

            def conv(g, n):
                rootT = (hT, hcT)[n]
                for h in range(2):
                    if n == 0:
                        pe.wait_ge(hT_sb, 9 * g + 7 + h + 1)
                    nc.tensor.matmul(psD[:, COLS[h]], conv_w[:, 2 * n, :], rootT[:, COLS[h]], start=True, stop=False)

                def neighbours(h, k, tiles):
                    for t in tiles:
                        last = nc.tensor.matmul(psA[:, COLS[h]], parts[:, k, t * P:(t + 1) * P], mask[:, t, COLS[h]],
                                                start=(k == 0 and t == 0), stop=(k == 2 and t == T - 1))
                    return last

                for k in range(2):
                    for s in range(2):
                        pe.wait_ge(part_sb, 12 * g + 6 * n + 2 * k + s + 1)
                        neighbours(0, k, TILES[s])
                        neighbours(1, k, TILES[s])
                pe.wait_ge(part_sb, 12 * g + 6 * n + 6)
                for h in range(2):
                    neighbours(h, 2, range(T)).then_inc(neigh_ps, 1)
                for h in range(2):
                    pe.wait_ge(neighT_sb, 4 * g + 2 * n + h + 1)
                    nc.tensor.matmul(psD[:, COLS[h]], conv_w[:, 2 * n + 1, :], aggT[:, COLS[h]], start=False, stop=True).then_inc(conv_ps, 1)
                for h in range(2):
                    pe.wait_ge(hc_ready, 4 * g + 2 * n + h + 1)
                    transpose_half(psB, hcT, h).then_inc(hc_ps, 1)

            def transpose_mask(g):
                pe.wait_ge(mask_ready, 3 * g + 1)
                for t in range(T):
                    if t >= 2:
                        pe.wait_ge(maskT_sb, 8 * g + t - 1)
                    for j in range(T):
                        last = nc.tensor.transpose(psDb[:, t % 2, j], mask[:, t, j * P:(j + 1) * P], ident_bf[:, :])
                    last.then_inc(maskT_ps, 1)

            def sum_pairs(g, batch):
                pe.wait_ge(idx_ready, 8 * g + SPARSE[batch][-1] + 1)
                if batch > 0:
                    pe.wait_ge(wanted_ready, 3 * g + batch)
                for t in SPARSE[batch]:
                    last = nc.tensor.matmul(pair_counts(t), ones_h[:, :], top[:, t, ALWAYS:SAMPLES:2], start=True, stop=True)
                last.then_inc(occupied_ps, 1)

            def attend(g, t):
                pe.wait_ge(probT_sb, 8 * g + t + 1)
                for j in range(T):
                    last = nc.tensor.matmul(psA[:, t * P:(t + 1) * P], probT[:, t % 2, j * P:(j + 1) * P], gn[:, j, :],
                                            start=(j == 0), stop=(j == T - 1))
                last.then_inc(ctx_done, 1)

            def iteration(g, q, ahead=True):
                pe.wait_ge(h0_ready, g + 1)
                pe.wait_ge(x_final, g + 1)
                transposes(psB, flat(h0[q][:, :, :]), ident[:, :]).then_inc(h0T_ps, 1)
                if ahead:
                    transpose_mask(g)
                pe.wait_ge(hT_sb, 9 * g + 1)
                for h in range(2):
                    nc.tensor.matmul(psA[:, COLS[h]], ones[0:1, :], b0_row[0:1, :], start=True, stop=False, skip_group_check=True)
                    for t in TILES[h]:
                        rows = slice(t * P, (t + 1) * P)
                        nc.tensor.matmul(psA[:, rows], hT[:, rows], w0[:, 0, :], start=False, stop=False, skip_group_check=True)
                pe.wait_ge(reduced, 8 * g + T)
                for h in range(2):
                    transpose_half(psC, flat(agg[:, :, :]), h).then_inc(aggT_ps, 1)
                for h in range(2):
                    pe.wait_ge(aggT_sb, 2 * g + h + 1)
                    for t in TILES[h]:
                        rows = slice(t * P, (t + 1) * P)
                        last = nc.tensor.matmul(psA[:, rows], aggT[:, rows], w0[:, 1, :], start=False, stop=True, skip_group_check=True)
                    last.then_inc(lin0_ps, 1)
                if not ahead:
                    transpose_mask(g)
                pe.wait_ge(maskT_sb, 8 * g + T)
                project(g, 0)
                if ahead:
                    sum_pairs(g + 1, 0)
                for t in range(T):
                    pe.wait_ge(prob_sb, 16 * g + t + 1)
                    pe.wait_ge(gz_ready, 8 * g + t + 1)
                    for h in range(N // HALF):
                        cols = slice(h * HALF, (h + 1) * HALF)
                        last = nc.tensor.matmul(psB[:, cols], gz[:, t % 2, :], prob[:, t % 2, cols], start=(t == 0), stop=(t == T - 1))
                    last.then_inc(pv_done, 1)
                for h in range(2):
                    pe.wait_ge(hT_sb, 9 * g + 3 + h + 1)
                    transpose_half(psC, hT, h).then_inc(att1_ps, 1)
                project(g, 1)
                if ahead:
                    sum_pairs(g + 1, 1)
                pe.wait_ge(proj_sb, 2 * g + 2)
                for t in range(T):
                    pe.wait_ge(prob_sb, 16 * g + 8 + t + 1)
                    if t >= 2:
                        pe.wait_ge(probT_sb, 8 * g + t - 1)
                    transposes((psB, psC)[t % 2], prob[:, t % 2, :], ident[:, :]).then_inc(probT_ps, 1)
                    if t >= 1:
                        attend(g, t - 1)
                attend(g, T - 1)
                pe.wait_ge(mask_ready, 3 * g + 3)
                for j in range(T):
                    for t in range(T):
                        last = nc.tensor.matmul(psD[:, T + j:T + j + 1], mask[:, t, j * P:(j + 1) * P], ones_bf[:, 0:1],
                                                start=(t == 0), stop=(t == T - 1))
                last.then_inc(degree_ps, 1)
                if ahead:
                    sum_pairs(g + 1, 2)
                for h in range(2):
                    pe.wait_ge(hn_ready, 6 * g + 4 + h + 1)
                    transpose_half(psB, flat(hn[:, :, :]), h).then_inc(hnT_ps, 1)
                pe.wait_ge(rdegree_ready, g + 1)
                for j in range(T):
                    last = nc.tensor.matmul(psC[:, j * P:(j + 1) * P], rdegree[:, j:j + 1].to_broadcast([P, P]), ident[:, :],
                                            start=True, stop=True)
                last.then_inc(ideg_ps, 1)
                conv(g, 0)
                conv(g, 1)

            for batch in range(3):
                sum_pairs(0, batch)
            with pe.Fori(0, (B - 2) // 2) as pair:
                for q in range(2):
                    iteration(pair * 2 + q, q)
            iteration(B - 2, 0)
            iteration(B - 1, 1, ahead=False)


_INS = ['x', 'adj', 'L0_gnn_W', 'L0_gnn_b', 'L1_gnn_W', 'L1_gnn_a', 'L2_gnn_W', 'L2_gnn_a', 'L3_gnn_w_rel1',
        'L3_gnn_w_root1', 'L3_gnn_b1', 'L3_gnn_w_rel2', 'L3_gnn_w_root2', 'L3_gnn_b2']
_OUTS = [((8, 1024, 128), 'float32')]


def kernel(**inputs):
    import numpy as _np
    import concourse.bacc as _bacc
    from concourse import mybir as _mybir
    from concourse.bass_utils import run_bass_kernel_spmd as _run

    nc = _bacc.Bacc("TRN2", target_bir_lowering=False, num_devices=1)
    arrays, args = {}, []
    for name in _INS:
        a = _np.ascontiguousarray(inputs[name])
        arrays[f"in_{name}_dram"] = a
        args.append(nc.dram_tensor(f"in_{name}_dram", a.shape, _mybir.dt.from_np(a.dtype), kind="ExternalInput").ap())
    for i, (shape, dtype) in enumerate(_OUTS):
        dt = _mybir.dt.from_np(_np.dtype(dtype))
        args.append(nc.dram_tensor(f"out_{i}_dram", shape, dt, kind="ExternalOutput").ap())
    gnn_stack(nc, *args)
    r = _run(nc, [arrays], core_ids=[0])
    return r.results[0]["out_0_dram"]
```
